# Optimizing a Trainium2 kernel written in Bass

```python
import numpy as np
import jax
import jax.numpy as jnp

def _softmax(x, axis=-1):
    return jax.nn.softmax(x, axis=axis)

def _gelu(x):
    return jax.nn.gelu(x, approximate=True)

def _silu(x):
    return jax.nn.silu(x)

def _sigmoid(x):
    return jax.nn.sigmoid(x)

def _layernorm(x, axis=-1, eps=1e-05):
    m = jnp.mean(x, axis=axis, keepdims=True)
    v = jnp.var(x, axis=axis, keepdims=True)
    return (x - m) / jnp.sqrt(v + eps)

def _scatter_add(tgt, idx, src, axis=0):
    return tgt.at[idx].add(src)

def _segment_sum(src, seg, n):
    return jax.ops.segment_sum(src, seg, n)
kernel_name = 'mk_hybrid_d1_jaxref_r8_abd712'

def setup_inputs(seed: int=0):
    np.random.seed(seed)
    _w = jnp.asarray

    def _L0_attn_a_setup():
        import jax, jax.numpy as jnp
        import numpy as np
        HIDDEN = 256
        N_HEADS = 16
        HEAD_DIM = HIDDEN // N_HEADS
        KV_DIM = HEAD_DIM
        INTER = 4 * HIDDEN
        EPS = 1e-05

        def _ln(x, g, b):
            m = jnp.mean(x, -1, keepdims=True)
            v = jnp.var(x, -1, keepdims=True)
            return (x - m) * jax.lax.rsqrt(v + EPS) * g + b

        def _block(x, ln1_g, ln1_b, ln2_g, ln2_b, wq, bq, wkv, bkv, wo, bo, wfc, bfc, wproj, bproj):
            B, S, H = x.shape
            scale = HEAD_DIM ** (-0.5)
            res = x
            h = _ln(x, ln1_g, ln1_b)
            q = (h @ wq + bq).reshape(B, S, N_HEADS, HEAD_DIM)
            kv = h @ wkv + bkv
            k, v = (kv[..., :KV_DIM], kv[..., KV_DIM:])
            scores = jnp.einsum('bshd,btd->bhst', q, k) * scale
            causal = jnp.tril(jnp.ones((S, S), bool))
            scores = jnp.where(causal, scores, jnp.finfo(scores.dtype).min)
            probs = jax.nn.softmax(scores, axis=-1)
            attn = jnp.einsum('bhst,btd->bshd', probs, v).reshape(B, S, H)
            x = attn @ wo + bo + res
            res = x
            h = _ln(x, ln2_g, ln2_b)
            h = jax.nn.gelu(h @ wfc + bfc, approximate=True)
            return h @ wproj + bproj + res
        key = jax.random.key(seed)
        ks = jax.random.split(key, 16)
        s = 0.02
        d = dict(hidden_states=jax.random.normal(ks[0], (4, 256, HIDDEN), jnp.float32), ln1_g=jnp.ones((HIDDEN,), jnp.float32), ln1_b=jnp.zeros((HIDDEN,), jnp.float32), ln2_g=jnp.ones((HIDDEN,), jnp.float32), ln2_b=jnp.zeros((HIDDEN,), jnp.float32), wq=jax.random.normal(ks[1], (HIDDEN, HIDDEN), jnp.float32) * s, bq=jnp.zeros((HIDDEN,), jnp.float32), wkv=jax.random.normal(ks[2], (HIDDEN, 2 * KV_DIM), jnp.float32) * s, bkv=jnp.zeros((2 * KV_DIM,), jnp.float32), wo=jax.random.normal(ks[3], (HIDDEN, HIDDEN), jnp.float32) * s, bo=jnp.zeros((HIDDEN,), jnp.float32), wfc=jax.random.normal(ks[4], (HIDDEN, INTER), jnp.float32) * s, bfc=jnp.zeros((INTER,), jnp.float32), wproj=jax.random.normal(ks[5], (INTER, HIDDEN), jnp.float32) * s, bproj=jnp.zeros((HIDDEN,), jnp.float32))
        return d
    _L0_attn_a_in = _L0_attn_a_setup()

    def _L0_attn_b_setup():
        import jax, jax.numpy as jnp
        import numpy as np
        B, S, H = (4, 256, 256)
        key = jax.random.key(seed)
        k1, k2, k3 = jax.random.split(key, 3)
        xav_qkv = float(np.sqrt(6.0 / (H + 3 * H)))
        xav_out = float(np.sqrt(6.0 / (H + H)))
        return {'hidden_states': jax.random.normal(k1, (B, S, H), dtype=jnp.float32), 'w_qkv': jax.random.uniform(k2, (3 * H, H), minval=-xav_qkv, maxval=xav_qkv, dtype=jnp.float32), 'b_qkv': jnp.zeros((3 * H,), dtype=jnp.float32), 'w_out': jax.random.uniform(k3, (H, H), minval=-xav_out, maxval=xav_out, dtype=jnp.float32), 'b_out': jnp.zeros((H,), dtype=jnp.float32)}
    _L0_attn_b_in = _L0_attn_b_setup()

    def _L0_ffn_setup():
        import jax, jax.numpy as jnp
        import numpy as np
        B, S, H, I = (1, 64, 256, 768)

        def _quantized_matmul(x, w, scale):
            wq = w.astype(jnp.float8_e4m3fn).astype(x.dtype)
            y = jnp.einsum('bsi,io->bso', x, wq)
            return y * scale
        key = jax.random.key(seed)
        ks = jax.random.split(key, 7)
        return {'x': jax.random.normal(ks[0], (B, S, H), dtype=jnp.float32), 'gate_w': jax.random.normal(ks[1], (H, I), dtype=jnp.float32) * 0.02, 'up_w': jax.random.normal(ks[2], (H, I), dtype=jnp.float32) * 0.02, 'down_w': jax.random.normal(ks[3], (I, H), dtype=jnp.float32) * 0.02, 'gate_scale': jax.random.uniform(ks[4], (I,), dtype=jnp.float32, minval=0.5, maxval=1.5), 'up_scale': jax.random.uniform(ks[5], (I,), dtype=jnp.float32, minval=0.5, maxval=1.5), 'down_scale': jax.random.uniform(ks[6], (H,), dtype=jnp.float32, minval=0.5, maxval=1.5)}
    _L0_ffn_in = _L0_ffn_setup()
    _d = {'L0_attn_a_hidden_states': _L0_attn_a_in['hidden_states'], 'L0_attn_a_ln1_g': _L0_attn_a_in['ln1_g'], 'L0_attn_a_ln1_b': _L0_attn_a_in['ln1_b'], 'L0_attn_a_ln2_g': _L0_attn_a_in['ln2_g'], 'L0_attn_a_ln2_b': _L0_attn_a_in['ln2_b'], 'L0_attn_a_wq': _L0_attn_a_in['wq'], 'L0_attn_a_bq': _L0_attn_a_in['bq'], 'L0_attn_a_wkv': _L0_attn_a_in['wkv'], 'L0_attn_a_bkv': _L0_attn_a_in['bkv'], 'L0_attn_a_wo': _L0_attn_a_in['wo'], 'L0_attn_a_bo': _L0_attn_a_in['bo'], 'L0_attn_a_wfc': _L0_attn_a_in['wfc'], 'L0_attn_a_bfc': _L0_attn_a_in['bfc'], 'L0_attn_a_wproj': _L0_attn_a_in['wproj'], 'L0_attn_a_bproj': _L0_attn_a_in['bproj'], 'L0_attn_b_w_qkv': _L0_attn_b_in['w_qkv'], 'L0_attn_b_b_qkv': _L0_attn_b_in['b_qkv'], 'L0_attn_b_w_out': _L0_attn_b_in['w_out'], 'L0_attn_b_b_out': _L0_attn_b_in['b_out'], 'L0_ffn_gate_w': _L0_ffn_in['gate_w'], 'L0_ffn_up_w': _L0_ffn_in['up_w'], 'L0_ffn_down_w': _L0_ffn_in['down_w'], 'L0_ffn_gate_scale': _L0_ffn_in['gate_scale'], 'L0_ffn_up_scale': _L0_ffn_in['up_scale'], 'L0_ffn_down_scale': _L0_ffn_in['down_scale']}
    _x0 = _d['L0_attn_a_hidden_states']
    _d['L0_attn_a_hidden_states'] = jax.random.normal(jax.random.fold_in(jax.random.key(seed), 1), (8, 256, 256), dtype=_x0.dtype)
    del _x0
    return _d

def reference(L0_attn_a_hidden_states, L0_attn_a_ln1_g, L0_attn_a_ln1_b, L0_attn_a_ln2_g, L0_attn_a_ln2_b, L0_attn_a_wq, L0_attn_a_bq, L0_attn_a_wkv, L0_attn_a_bkv, L0_attn_a_wo, L0_attn_a_bo, L0_attn_a_wfc, L0_attn_a_bfc, L0_attn_a_wproj, L0_attn_a_bproj, L0_attn_b_w_qkv, L0_attn_b_b_qkv, L0_attn_b_w_out, L0_attn_b_b_out, L0_ffn_gate_w, L0_ffn_up_w, L0_ffn_down_w, L0_ffn_gate_scale, L0_ffn_up_scale, L0_ffn_down_scale):

    def _L0_attn_a_ref(hidden_states, ln1_g, ln1_b, ln2_g, ln2_b, wq, bq, wkv, bkv, wo, bo, wfc, bfc, wproj, bproj):
        import jax, jax.numpy as jnp
        import numpy as np
        HIDDEN = 256
        N_HEADS = 16
        HEAD_DIM = HIDDEN // N_HEADS
        KV_DIM = HEAD_DIM
        INTER = 4 * HIDDEN
        EPS = 1e-05

        def _ln(x, g, b):
            m = jnp.mean(x, -1, keepdims=True)
            v = jnp.var(x, -1, keepdims=True)
            return (x - m) * jax.lax.rsqrt(v + EPS) * g + b

        def _block(x, ln1_g, ln1_b, ln2_g, ln2_b, wq, bq, wkv, bkv, wo, bo, wfc, bfc, wproj, bproj):
            B, S, H = x.shape
            scale = HEAD_DIM ** (-0.5)
            res = x
            h = _ln(x, ln1_g, ln1_b)
            q = (h @ wq + bq).reshape(B, S, N_HEADS, HEAD_DIM)
            kv = h @ wkv + bkv
            k, v = (kv[..., :KV_DIM], kv[..., KV_DIM:])
            scores = jnp.einsum('bshd,btd->bhst', q, k) * scale
            causal = jnp.tril(jnp.ones((S, S), bool))
            scores = jnp.where(causal, scores, jnp.finfo(scores.dtype).min)
            probs = jax.nn.softmax(scores, axis=-1)
            attn = jnp.einsum('bhst,btd->bshd', probs, v).reshape(B, S, H)
            x = attn @ wo + bo + res
            res = x
            h = _ln(x, ln2_g, ln2_b)
            h = jax.nn.gelu(h @ wfc + bfc, approximate=True)
            return h @ wproj + bproj + res
        return _block(hidden_states, ln1_g, ln1_b, ln2_g, ln2_b, wq, bq, wkv, bkv, wo, bo, wfc, bfc, wproj, bproj)

    def _L0_attn_b_ref(hidden_states, w_qkv, b_qkv, w_out, b_out):
        import jax, jax.numpy as jnp
        import numpy as np
        B, S, H = (4, 256, 256)
        Bc, Sc, Hc = hidden_states.shape
        scaling = jnp.sqrt(jnp.asarray(Hc, hidden_states.dtype))
        qkv = jnp.einsum('bsh,oh->bso', hidden_states, w_qkv) + b_qkv
        q, k, v = jnp.split(qkv, 3, axis=-1)
        scores = jnp.einsum('bqh,bkh->bqk', q, k) / scaling
        probs = jax.nn.softmax(scores, axis=-1)
        context = jnp.einsum('bqk,bkh->bqh', probs, v)
        out = jnp.einsum('bsh,oh->bso', context, w_out) + b_out
        return out

    def _L0_ffn_ref(x, gate_w, up_w, down_w, gate_scale, up_scale, down_scale):
        import jax, jax.numpy as jnp
        import numpy as np
        B, S, H, I = (1, 64, 256, 768)

        def _quantized_matmul(x, w, scale):
            wq = w.astype(jnp.float8_e4m3fn).astype(x.dtype)
            y = jnp.einsum('bsi,io->bso', x, wq)
            return y * scale
        gate = jax.nn.silu(_quantized_matmul(x, gate_w, gate_scale))
        up = _quantized_matmul(x, up_w, up_scale)
        fuse = gate * up
        return _quantized_matmul(fuse, down_w, down_scale)
    x = L0_attn_a_hidden_states
    x = x + _L0_attn_a_ref(_layernorm(x, axis=-1), L0_attn_a_ln1_g, L0_attn_a_ln1_b, L0_attn_a_ln2_g, L0_attn_a_ln2_b, L0_attn_a_wq, L0_attn_a_bq, L0_attn_a_wkv, L0_attn_a_bkv, L0_attn_a_wo, L0_attn_a_bo, L0_attn_a_wfc, L0_attn_a_bfc, L0_attn_a_wproj, L0_attn_a_bproj)
    x = x + _L0_ffn_ref(_layernorm(x, axis=-1), L0_ffn_gate_w, L0_ffn_up_w, L0_ffn_down_w, L0_ffn_gate_scale, L0_ffn_up_scale, L0_ffn_down_scale)
    x = x + _L0_attn_b_ref(_layernorm(x, axis=-1), L0_attn_b_w_qkv, L0_attn_b_b_qkv, L0_attn_b_w_out, L0_attn_b_b_out)
    x = x + _L0_ffn_ref(_layernorm(x, axis=-1), L0_ffn_gate_w, L0_ffn_up_w, L0_ffn_down_w, L0_ffn_gate_scale, L0_ffn_up_scale, L0_ffn_down_scale)
    return x

_drawn_inputs = setup_inputs


def setup_inputs(seed=0):
    import zlib

    import numpy as np

    out = dict(_drawn_inputs(seed))
    spreads = {'L0_attn_a_ln1_g': (1.0, 0.6),
     'L0_attn_a_ln1_b': (0.0, 0.8),
     'L0_attn_a_ln2_g': (1.0, 0.6),
     'L0_attn_a_ln2_b': (0.0, 0.8),
     'L0_attn_a_bq': (0.0, 0.8),
     'L0_attn_a_bkv': (0.0, 0.506),
     'L0_attn_a_bo': (0.0, 0.1),
     'L0_attn_a_bfc': (0.0, 0.447),
     'L0_attn_a_bproj': (0.0, 0.1),
     'L0_attn_b_b_qkv': (0.0, 0.591),
     'L0_attn_b_b_out': (0.0, 0.613)}
    factors = {'L0_attn_a_wq': 8.0,
     'L0_attn_a_wkv': 5.479,
     'L0_attn_a_wo': 3.366,
     'L0_ffn_gate_scale': 5.363,
     'L0_ffn_up_scale': 6.179,
     'L0_ffn_down_scale': 6.005}
    for name, (base, spread) in spreads.items():
        noise = np.random.default_rng([zlib.crc32(name.encode()), seed]).standard_normal(out[name].shape)
        drawn = base * np.exp(spread * noise) if base else spread * noise
        out[name] = jnp.asarray(drawn.astype(out[name].dtype))
    for name, factor in factors.items():
        out[name] = (out[name] * factor).astype(out[name].dtype)
    return out
```

```python
from contextlib import ExitStack

import concourse.bass as bass
from concourse import mybir

ALU = mybir.AluOpType
ACT = mybir.ActivationFunctionType
AX_X = mybir.AxisListType.X
F32 = mybir.dt.float32
F32R = mybir.dt.float32r
BF16 = mybir.dt.bfloat16
I32 = mybir.dt.int32

P = 128
BATCH, S, H = 8, 256, 256
HEADS, HD = 16, 16
INTER, FF = 1024, 768
KT = H // P
TT = S // P
MT_FC = INTER // P
MT_FF = FF // P
SIDES = 2
TURNS = BATCH // SIDES
EPS = 1e-5
BANKS = 8
HGROUPS = HEADS // 4
LOADS = 21
STACK = 96
NEG = -3.0e38

STAGES = ["ln0", "ln1", "tr1", "q", "kv", "vt", "smax", "mt", "st", "pv", "wo",
          "ln2", "tr2", "fc", "proj", "ln3", "tr3", "gu1", "down1",
          "ln4", "tr4", "qb", "kb", "vb", "sb", "pt", "ctx", "out",
          "ln5", "tr5", "gu2", "down2"]
ORDER = [(stage, side) for stage in STAGES for side in range(SIDES)]
FILLS = {"tr1": 1, "q": 1, "kv": 1, "vt": 1, "smax": 12, "mt": 1, "st": 12, "pv": 2, "wo": 1,
         "tr2": 1, "fc": MT_FC // 2, "proj": 1, "tr3": 1, "gu1": MT_FF, "down1": 1,
         "tr4": 1, "qb": 1, "kb": 1, "vb": 1, "sb": 1, "pt": 1, "ctx": 1, "out": 1,
         "tr5": 1, "gu2": MT_FF, "down2": 1}
FILL_NO = {}
for _stage, _side in ORDER:
    for _i in range(FILLS.get(_stage, 0)):
        FILL_NO[(_stage, _side, _i)] = len(FILL_NO)
FILL_AT = {n: key for key, n in FILL_NO.items()}
USES = [len([n for n in FILL_NO.values() if n % BANKS == b]) for b in range(BANKS)]


COLUMNS = [("ln1_g", KT), ("ln1_b", KT), ("ln2_g", KT), ("ln2_b", KT), ("bq", KT), ("bkv", 1),
           ("bfc", MT_FC), ("bqkb", 2 * KT), ("gate_scale", MT_FF), ("up_scale", MT_FF)]
ROWS = ["bo", "bproj", "bvb", "bout", "down_scale"]


def build(nc, x, columns, rows, wq, wkv, wo, wfc, wproj, w_qkv_t, w_out_t, gate_w, up_w, down_w, out):
    ctx = ExitStack()
    with ctx:
        def sb(name, shape, dt=F32):
            return ctx.enter_context(nc.sbuf_tensor(name, shape, dt))

        def sem(name):
            return ctx.enter_context(nc.semaphore(name))

        class Count:

            def __init__(self, name, per_turn, each=1, before=0):
                self.sem, self.per_turn, self.each, self.before = sem(name), per_turn, each, before

            def at(self, turn, k):
                return turn * (self.per_turn * self.each) + (k * self.each + self.before)

        def sides(name, per_turn, each=1, before=0):
            return [Count(f"{name}{s}", per_turn, each, before) for s in range(SIDES)]

        wq_r = [sb(f"wq_{n}", [P, KT, H], F32R) for n in ("hi", "lo")]
        wkv_r = [sb(f"wkv_{n}", [P, KT, STACK], F32R) for n in ("hi", "lo")]
        wo_r = [sb(f"wo_{n}", [P, HGROUPS, H], F32R) for n in ("hi", "lo")]
        wfc_r = [sb(f"wfc_{n}", [P, KT, INTER], F32R) for n in ("hi", "lo")]
        wproj_r = [sb(f"wproj_{n}", [P, MT_FC, H], F32R) for n in ("hi", "lo")]
        wqkvb_r = [sb(f"wqkvb_{n}", [P, KT, 3 * H], F32R) for n in ("hi", "lo")]
        wout_r = [sb(f"wout_{n}", [P, KT, H], F32R) for n in ("hi", "lo")]
        gate8 = sb("gate8", [P, KT, FF], F32R)
        up8 = sb("up8", [P, KT, FF], F32R)
        down8 = sb("down8", [P, MT_FF, H], F32R)

        col_table = sb("columns", [P, sum(n for _, n in COLUMNS)])
        row_table = sb("rows", [P, len(ROWS), H])
        col, at = {}, 0
        for name, n in COLUMNS:
            col[name] = col_table[:, at:at + n]
            at += n
        row = {name: row_table[:, r, :] for r, name in enumerate(ROWS)}

        ident = sb("ident", [P, P])
        ident_b = sb("ident_b", [P, P], BF16)
        causal_b = sb("causal_b", [P, P], BF16)
        neg_half = sb("neg_half", [P, TT])

        def each_side(name, shape, dt=F32):
            return [sb(f"{name}{s}", shape, dt) for s in range(SIDES)]

        x_in = each_side("x_in", [P, TT, H])
        cur = each_side("cur", [P, TT, H])
        h = each_side("h", [P, TT, H])
        base = each_side("base", [P, TT, H])
        in_full = each_side("in_full", [P, KT, S])
        in_hi = each_side("in_hi", [P, KT, S], F32R)
        in_lo = each_side("in_lo", [P, KT, S], F32R)
        wide = each_side("wide", [P, 24 * S])
        mid = each_side("mid", [P, 16 * S], F32R)
        kst = each_side("kst", [STACK, 2, S], F32R)
        vaug = each_side("vaug", [P, TT, 32])
        m = each_side("m", [P, TT, HEADS])
        attmp = each_side("attmp", [P, 2, 2 * S])
        bnst = each_side("bnst", [P, TT, 6])
        mv = each_side("mv", [P, TT, 2])
        veps = each_side("veps", [P, TT])
        rstd = each_side("rstd", [P, TT])
        mb = each_side("mb", [P, TT])
        nmb = each_side("nmb", [P, TT])
        sumb = each_side("sumb", [P, TT])
        rsumb = each_side("rsumb", [P, TT])

        qst = [mid[s][:, :].rearrange("p (h s) -> p h s", h=HEADS) for s in range(SIDES)]
        mrow = [in_lo[s][0:HEADS, :, :] for s in range(SIDES)]
        mid_hi = [mid[s][:, 0:8 * S] for s in range(SIDES)]
        mid_lo = [mid[s][:, 8 * S:16 * S] for s in range(SIDES)]
        q_scr = nc.dram_tensor("q_scr", (SIDES, 2, H, S), F32, kind="Internal").ap()

        m_scr = nc.dram_tensor("m_scr", (SIDES, 2, HEADS, S), F32, kind="Internal").ap()

        ps = [ctx.enter_context(nc.psum_tensor(f"bank{b}", [P, 512], F32)) for b in range(BANKS)]

        loaded = sem("weights_loaded")
        x_loaded = sides("x_loaded", 1, 16)
        x_in_free = sides("x_in_free", 1)
        stored = sides("stored", 1, 16, before=16)
        const_ready = sem("const_ready")
        prep = sem("prep")
        prep_hi = sem("prep_hi")
        prep_pool = sem("prep_pool")
        passed = sem("passed")
        bank_full = [sem(f"bank_full{b}") for b in range(BANKS)]
        VLINKS, ALINKS, GLINKS = 28, 2, 14
        vlink = Count("vector_step", VLINKS)
        alink = Count("scalar_step", ALINKS)
        glink = Count("pool_step", GLINKS)

        stats = sides("stats", 6)
        rstd_ok = sides("rstd_ok", 6)
        normed = sides("normed", 6)
        affine = sides("affine", 2)
        inhi = sides("inhi", 5)
        inlo = sides("inlo", 5)
        qhi = sides("qhi", 1)
        qlo = sides("qlo", 1)
        q_out = sides("q_out", 2, 16)
        q_stack = sides("q_stack", 4, 16)
        kvfull = sides("kvfull", 1)
        khi = sides("khi", 1)
        klo = sides("klo", 1)
        v_ok = sides("v_ok", 1)
        max_ok = sides("max_ok", 12)
        mhi = sides("mhi", 1)
        mlo = sides("mlo", 1)
        m_out = sides("m_out", 1, 16)
        m_rows = sides("m_rows", 1, 16)
        exped = sides("exped", 12)
        masked = sides("masked", 12)
        att_full = sides("att_full", 2)
        att_hi = sides("att_hi", 2)
        att_lo = sides("att_lo", 2)
        base_ok = sides("base_ok", 3)
        summed = sides("summed", 4)
        out_ok = sides("out_ok", 1)
        gelu = sides("gelu", 4)
        gelu_hi = sides("gelu_hi", 4)
        gelu_lo = sides("gelu_lo", 4)
        silu = sides("silu", 2 * MT_FF)
        fused = sides("fused", 2 * MT_FF)
        fuse_hi = sides("fuse_hi", 2 * MT_FF)
        fuse_lo = sides("fuse_lo", 2 * MT_FF)
        qkb_full = sides("qkb_full", 2)
        qkb_hi = sides("qkb_hi", 2)
        qkb_lo = sides("qkb_lo", 2)
        vb_full = sides("vb_full", 1)
        vb_hi = sides("vb_hi", 1)
        vb_lo = sides("vb_lo", 1)
        sb_max = sides("sb_max", 1)
        sb_exp = sides("sb_exp", 1)
        sb_norm = sides("sb_norm", 1)
        pt_hi = sides("pt_hi", 1)
        pt_lo = sides("pt_lo", 1)
        ctx_hi = sides("ctx_hi", 1)
        ctx_lo = sides("ctx_lo", 1)

        def bank_of(stage, s, i=0):
            return ps[FILL_NO[(stage, s, i)] % BANKS]

        def fills_of(stage, s, i=0):
            return bank_full[FILL_NO[(stage, s, i)] % BANKS]

        def filled(turn, stage, s, i=0):
            n = FILL_NO[(stage, s, i)]
            return bank_full[n % BANKS], turn * USES[n % BANKS] + (n // BANKS + 1)

        def last_read(stage, s, i):
            f = MT_FF * (stage == "gu2")
            return {"tr1": (affine[s], 1), "tr2": (affine[s], 2), "tr3": (inlo[s], 3), "tr4": (inlo[s], 4),
                    "tr5": (inlo[s], 5), "q": (qhi[s], 1), "kv": (kvfull[s], 1), "vt": (v_ok[s], 1),
                    "smax": (max_ok[s], i + 1), "mt": (mlo[s], 1), "st": (exped[s], i + 1),
                    "pv": (att_full[s], i + 1), "wo": (summed[s], 1), "proj": (summed[s], 2),
                    "fc": (gelu[s], i + 1), "gu1": (fused[s], i + 1), "gu2": (fused[s], f + i + 1),
                    "down1": (summed[s], 3), "qb": (qkb_full[s], 1), "kb": (qkb_full[s], 2),
                    "vb": (vb_full[s], 1), "sb": (sb_exp[s], 1), "pt": (pt_lo[s], 1),
                    "ctx": (ctx_lo[s], 1), "out": (summed[s], 4), "down2": (out_ok[s], 1)}[stage]

        def emptied(turn, stage, s, i=0):
            n = FILL_NO[(stage, s, i)]
            if n < BANKS:
                return const_ready, 2
            count, k = last_read(*FILL_AT[n - BANKS])
            return count.sem, count.at(turn, k)

        raw_at = {}
        at = 0
        for name, n in (("wq", 512), ("wkv", 2 * STACK), ("wo", 1024), ("wfc", 2048), ("wproj", 2048)):
            raw_at[name] = wide[0][:, at:at + n]
            at += n
        at = 0
        for name, n in (("wqkvb", 1536), ("wout", 512), ("gate", 1536), ("up", 1536)):
            raw_at[name] = wide[1][:, at:at + n]
            at += n
        raw_down = [attmp[0], attmp[1]]
        grid = wide[1][:, 5120:5120 + 768]

        block = ctx.enter_context(nc.Block())

        @block.sync
        def _(sp):
            loads = []

            def load(dst, src):
                loads.append(dst)
                sp.dma_start(dst, src).then_inc(loaded, 16)

            def as3(ap, a):
                return ap.rearrange("p (a n) -> p a n", a=a)

            for s in range(SIDES):
                sp.dma_start(x_in[s][:, :, :], x[s].rearrange("(i p) n -> p i n", p=P))\
                    .then_inc(x_loaded[s].sem, 16)
            load(col_table[:, :], columns)
            load(row_table[:, :, :], rows.partition_broadcast(P))
            load(as3(raw_at["wq"], KT), wq.rearrange("(k p) n -> p k n", p=P))
            wkv_v = wkv.rearrange("(k p) n -> p k n", p=P)
            for r in range(6):
                part = wkv_v[:, :, 0:HD] if r < 4 else wkv_v[:, :, HD:2 * HD]
                load(as3(raw_at["wkv"], KT)[:, :, 16 * r:16 * r + 16], part)
            wo_v = wo.rearrange("(g j d) n -> j d g n", j=4, d=HD)
            sp.wait_ge(const_ready, 1)
            for j in range(4):
                load(as3(raw_at["wo"], HGROUPS)[32 * j:32 * j + HD], wo_v[j])
            load(as3(raw_at["wfc"], KT), wfc.rearrange("(k p) n -> p k n", p=P))
            load(as3(raw_at["wproj"], MT_FC), wproj.rearrange("(k p) n -> p k n", p=P))
            load(as3(raw_at["gate"], KT), gate_w.rearrange("(k p) n -> p k n", p=P))
            load(as3(raw_at["up"], KT), up_w.rearrange("(k p) n -> p k n", p=P))
            for c in range(2):
                load(raw_down[c][:, :, :].rearrange("p a n -> p (a n)")[:, 0:768].rearrange("p (a n) -> p a n", a=3),
                     down_w.rearrange("(k p) n -> p k n", p=P)[:, 3 * c:3 * c + 3, :])
            load(as3(raw_at["wqkvb"], KT), w_qkv_t.rearrange("(k p) n -> p k n", p=P))
            load(as3(raw_at["wout"], KT), w_out_t.rearrange("(k p) n -> p k n", p=P))

            assert len(loads) == LOADS, len(loads)

            def one_turn(turn, more):
                for stage, s in ORDER:
                    if stage == "kv":
                        sp.wait_ge(qhi[s].sem, qhi[s].at(turn, 1))
                        sp.dma_start(q_scr[s, 0].rearrange("(k p) n -> p k n", p=P),
                                     wide[s][:, 512:1024].rearrange("p (k n) -> p k n", k=KT))\
                            .then_inc(q_out[s].sem, 16)
                        sp.wait_ge(qlo[s].sem, qlo[s].at(turn, 1))
                        sp.dma_start(q_scr[s, 1].rearrange("(k p) n -> p k n", p=P),
                                     wide[s][:, 1024:1536].rearrange("p (k n) -> p k n", k=KT))\
                            .then_inc(q_out[s].sem, 16)
                        sp.wait_ge(q_out[s].sem, q_out[s].at(turn, 2))
                        for r in range(4):
                            sp.dma_start(qst[s][16 * r:16 * r + 16, :, :].bitcast(F32),
                                         q_scr[s, r % 2].rearrange("(h d) n -> d h n", d=HD))\
                                .then_inc(q_stack[s].sem, 16)
                    if stage == "mt":
                        sp.wait_ge(mlo[s].sem, mlo[s].at(turn, 1))
                        sp.dma_start(m_scr[s].rearrange("c h n -> h c n"), mrow[s].bitcast(F32))\
                            .then_inc(m_out[s].sem, 16)
                        sp.wait_ge(m_out[s].sem, m_out[s].at(turn, 1))
                        sp.dma_start(mid[s][64:66, :].bitcast(F32), m_scr[s].rearrange("c h n -> c (h n)"))\
                            .then_inc(m_rows[s].sem, 16)
                    if stage == "gu1" and more:
                        sp.wait_ge(x_in_free[s].sem, x_in_free[s].at(turn, 1))
                        nxt = turn * SIDES + (SIDES + s)
                        sp.dma_start(x_in[s][:, :, :], x[bass.ds(nxt, 1)].rearrange("a (i p) n -> p (a i) n", p=P))\
                            .then_inc(x_loaded[s].sem, 16)
                    if stage == "down2":
                        sp.wait_ge(out_ok[s].sem, out_ok[s].at(turn, 1))
                        sp.dma_start(out[bass.ds(turn * SIDES + s, 1)].rearrange("a (i p) n -> p (a i) n", p=P),
                                     h[s][:, :, :]).then_inc(stored[s].sem, 16)

            with sp.Fori(0, TURNS - 1) as turn:
                one_turn(turn, True)
            one_turn(TURNS - 1, False)
            for s in range(SIDES):
                sp.wait_ge(stored[s].sem, 16 * (TURNS + 1))

        @block.gpsimd
        def _(pool):
            pool.memset(raw_at["wo"], 0.0).then_inc(const_ready, 1)
            pool.memset(ident[:, :], 0.0)
            pool.memset(ident_b[:, :], 0.0)
            pool.memset(causal_b[:, :], 0.0)
            for s in range(SIDES):
                pool.memset(vaug[s][:, :, :], 1.0)
            pool.memset(neg_half[:, :], -0.5).then_inc(prep_pool, 1)
            pool.wait_ge(prep_pool, 1)
            for t in (ident, ident_b):
                pool.affine_select(out=t[:, :], in_=t[:, :], compare_op=ALU.not_equal, fill=1.0, base=0,
                                   pattern=[[-1, P]], channel_multiplier=1)
            pool.affine_select(out=causal_b[:, :], in_=causal_b[:, :], compare_op=ALU.is_ge, fill=NEG, base=0,
                               pattern=[[-1, P]], channel_multiplier=1).then_inc(const_ready, 1)
            pool.wait_ge(const_ready, 2)

            steps = [0]

            with pool.Fori(0, TURNS) as turn:
                def link(ins):
                    steps[0] += 1
                    ins.then_inc(glink.sem, 1)
                    pool.wait_ge(glink.sem, glink.at(turn, steps[0]))
                    pool.sem_inc(passed, 1)

                def add_row(s, src, name):
                    return pool.tensor_tensor(base[s][:, :, :], src[s][:, :, :],
                                              row[name].unsqueeze(1).broadcast_to([P, TT, H]), ALU.add)

                for stage, s in ORDER:
                    if stage.startswith("ln"):
                        n = int(stage[2])
                        pool.wait_ge(stats[s].sem, stats[s].at(turn, n + 1))
                        pool.sem_inc(passed, 1)
                        link(pool.tensor_scalar(veps[s][:, :], mv[s][:, :, 1], EPS, None, ALU.add))
                        pool.tensor_tensor(rstd[s][:, :], veps[s][:, :], neg_half[:, :], ALU.pow)\
                            .then_inc(rstd_ok[s].sem, 1)
                    if stage == "tr1":
                        if s == 0:
                            pool.wait_ge(loaded, 16 * LOADS)
                        pool.wait_ge(normed[s].sem, normed[s].at(turn, 1))
                        pool.sem_inc(passed, 1)
                        add_row(s, cur, "bo").then_inc(base_ok[s].sem, 1)
                    if stage == "tr2":
                        pool.wait_ge(summed[s].sem, summed[s].at(turn, 1))
                        pool.sem_inc(passed, 1)
                        link(add_row(s, cur, "bproj"))
                        pool.wait_ge(x_loaded[s].sem, x_loaded[s].at(turn, 1))
                        pool.sem_inc(passed, 1)
                        ins = pool.tensor_tensor(base[s][:, :, :], base[s][:, :, :], x_in[s][:, :, :], ALU.add)
                        ins.then_inc(base_ok[s].sem, 1)
                        pool.wait_ge(base_ok[s].sem, base_ok[s].at(turn, 2))
                        pool.sem_inc(x_in_free[s].sem, 1)
                    if stage == "tr4":
                        pool.wait_ge(summed[s].sem, summed[s].at(turn, 3))
                        pool.sem_inc(passed, 1)
                        add_row(s, cur, "bout").then_inc(base_ok[s].sem, 1)
                    if stage == "st":
                        for i in range(12):
                            pool.wait_ge(exped[s].sem, exped[s].at(turn, i + 1))
                            pool.sem_inc(passed, 1)
                            if i < 8:
                                v = wide[s][:, 512 * i:512 * i + 512].rearrange("p (h n) -> p h n", h=2)[:, :, 0:P]
                                nh = 2
                            else:
                                v = wide[s][:, 512 * i:512 * i + 512].rearrange("p (h n) -> p h n", h=4)
                                nh = 4
                            pool.affine_select(out=v, in_=v, compare_op=ALU.is_ge, fill=0.0, base=0,
                                               pattern=[[0, nh], [1, P]], channel_multiplier=-1)\
                                .then_inc(masked[s].sem, 1)
                    if stage == "fc":
                        for i in range(4):
                            pool.wait_ge(gelu[s].sem, gelu[s].at(turn, i + 1))
                            pool.sem_inc(passed, 1)
                            pool.tensor_copy(mid_hi[s][:, 512 * i:512 * i + 512], wide[s][:, 512 * i:512 * i + 512])\
                                .then_inc(gelu_hi[s].sem, 1)
                    if stage in ("gu1", "gu2"):
                        f = MT_FF * (stage == "gu2")
                        for i in range(MT_FF):
                            pool.wait_ge(fused[s].sem, fused[s].at(turn, f + i + 1))
                            pool.sem_inc(passed, 1)
                            pool.tensor_copy(mid_hi[s][:, S * i:S * i + S], wide[s][:, S * i:S * i + S])\
                                .then_inc(fuse_hi[s].sem, 1)
            assert steps[0] == GLINKS, steps

        @block.scalar
        def _(act):
            act.wait_ge(loaded, 16 * LOADS)
            pairs = [(wq_r, "wq"), (wkv_r, "wkv"), (wo_r, "wo"), (wfc_r, "wfc"), (wproj_r, "wproj"),
                     (wqkvb_r, "wqkvb"), (wout_r, "wout")]
            for r, name in pairs:
                act.activation(r[0][:, :, :].rearrange("p a n -> p (a n)"), raw_at[name], ACT.Copy).then_inc(prep_hi, 1)
            steps = [0]

            with act.Fori(0, TURNS) as turn:
                def link(ins):
                    steps[0] += 1
                    ins.then_inc(alink.sem, 1)
                    act.wait_ge(alink.sem, alink.at(turn, steps[0]))

                for stage, s in ORDER:
                    if stage.startswith("tr"):
                        n = int(stage[2])
                        if n <= 2:
                            act.wait_ge(affine[s].sem, affine[s].at(turn, n))
                            src = in_full[s][:, :, :]
                        else:
                            act.wait_ge(*filled(turn, stage, s))
                            src = bank_of(stage, s)[:, :].rearrange("p (k n) -> p k n", k=KT)
                        act.activation(in_hi[s][:, :, :], src, ACT.Copy).then_inc(inhi[s].sem, 1)
                    if stage == "q":
                        act.wait_ge(*filled(turn, stage, s))
                        bank = bank_of(stage, s)
                        for k in range(KT):
                            ins = act.activation(wide[s][:, S * k:S * k + S], bank[:, S * k:S * k + S],
                                                 ACT.Identity, bias=col["bq"][:, k:k + 1])
                        link(ins)
                        act.activation(wide[s][:, 512:1024].bitcast(F32R), wide[s][:, 0:512], ACT.Copy)\
                            .then_inc(qhi[s].sem, 1)
                    if stage == "kv":
                        act.wait_ge(*filled(turn, stage, s))
                        bank = bank_of(stage, s)
                        full = wide[s][0:STACK, 1536:1536 + S]
                        act.activation(full, bank[0:STACK, 0:S], ACT.Identity, bias=col["bkv"][0:STACK, :])\
                            .then_inc(kvfull[s].sem, 1)
                        act.wait_ge(kvfull[s].sem, kvfull[s].at(turn, 1))
                        act.activation(kst[s][0:32, :, :], wide[s][0:32, 1536:1536 + S].unsqueeze(1).broadcast_to([32, 2, S]),
                                       ACT.Copy)
                        act.activation(wide[s][32:64, 1792:1792 + S].bitcast(F32R), wide[s][32:64, 1536:1536 + S],
                                       ACT.Copy).then_inc(khi[s].sem, 1)
                    if stage == "mt":
                        act.wait_ge(*filled(turn, stage, s))
                        bank = bank_of(stage, s)
                        act.activation(mrow[s][:, 0, :], bank[0:HEADS, 0:S], ACT.Copy, scale=-1.0)\
                            .then_inc(mhi[s].sem, 1)
                    if stage == "st":
                        for i in range(12):
                            act.wait_ge(*filled(turn, stage, s, i))
                            bank = bank_of(stage, s, i)
                            act.activation(wide[s][:, 512 * i:512 * i + 512], bank[:, :], ACT.Exp, scale=HD ** -0.5)\
                                .then_inc(exped[s].sem, 1)
                    if stage == "pv":
                        for c in range(2):
                            act.wait_ge(att_full[s].sem, att_full[s].at(turn, c + 1))
                            act.activation(mid_hi[s][:, 512 * c:512 * c + 512], attmp[s][:, 0, :], ACT.Copy)\
                                .then_inc(att_hi[s].sem, 1)
                    if stage == "fc":
                        for i in range(4):
                            act.wait_ge(*filled(turn, stage, s, i))
                            bank = bank_of(stage, s, i)
                            for j in range(2):
                                t = 2 * i + j
                                ins = act.activation(wide[s][:, S * t:S * t + S], bank[:, S * j:S * j + S],
                                                     ACT.Gelu_apprx_tanh, bias=col["bfc"][:, t:t + 1])
                            ins.then_inc(gelu[s].sem, 1)
                    if stage in ("gu1", "gu2"):
                        for i in range(MT_FF):
                            act.wait_ge(*filled(turn, stage, s, i))
                            bank = bank_of(stage, s, i)
                            act.activation(wide[s][:, 2048 + S * i:2048 + S * i + S], bank[:, 0:S], ACT.Silu,
                                           scale=col["gate_scale"][:, i:i + 1]).then_inc(silu[s].sem, 1)
                    if stage in ("qb", "kb"):
                        k = int(stage == "kb")
                        act.wait_ge(*filled(turn, stage, s))
                        bank = bank_of(stage, s)
                        for j in range(KT):
                            ins = act.activation(wide[s][:, 512 * k + S * j:512 * k + S * j + S], bank[:, S * j:S * j + S],
                                                 ACT.Identity, bias=col["bqkb"][:, KT * k + j:KT * k + j + 1])
                        ins.then_inc(qkb_full[s].sem, 1)
                        act.wait_ge(qkb_full[s].sem, qkb_full[s].at(turn, k + 1))
                        act.activation(mid_hi[s][:, 512 * k:512 * k + 512], wide[s][:, 512 * k:512 * k + 512], ACT.Copy)\
                            .then_inc(qkb_hi[s].sem, 1)
                    if stage == "vb":
                        act.wait_ge(vb_full[s].sem, vb_full[s].at(turn, 1))
                        act.activation(mid_hi[s][:, 1024:1536], wide[s][:, 1024:1536], ACT.Copy)\
                            .then_inc(vb_hi[s].sem, 1)
                    if stage == "sb":
                        act.wait_ge(*filled(turn, stage, s))
                        bank = bank_of(stage, s)
                        act.wait_ge(sb_max[s].sem, sb_max[s].at(turn, 1))
                        for i in range(TT):
                            ins = act.activation(wide[s][:, 4096 + S * i:4096 + S * i + S], bank[:, S * i:S * i + S],
                                                 ACT.Exp, bias=nmb[s][:, i:i + 1], scale=H ** -0.5,
                                                 accum_out=sumb[s][:, i:i + 1])
                        ins.then_inc(sb_exp[s].sem, 1)
                    if stage == "pt":
                        act.wait_ge(*filled(turn, stage, s))
                        bank = bank_of(stage, s)
                        act.activation(mid_hi[s][:, 1536:2048], bank[:, :], ACT.Copy).then_inc(pt_hi[s].sem, 1)
                    if stage == "ctx":
                        act.wait_ge(*filled(turn, stage, s))
                        bank = bank_of(stage, s)
                        act.activation(in_hi[s][:, :, :].rearrange("p k n -> p (k n)"), bank[:, :], ACT.Copy)\
                            .then_inc(ctx_hi[s].sem, 1)
            assert steps[0] == ALINKS, steps

        @block.vector
        def _(dve):
            done = [0]

            def then(ins):
                done[0] += 1
                ins.then_inc(prep, 1)
                dve.wait_ge(prep, done[0])

            for s in range(SIDES):
                then(dve.memset(kst[s][64:96, :, :].bitcast(F32), 0.0))
                then(dve.memset(kst[s][64:66, 1, :].bitcast(F32), 1.0))
                then(dve.memset(mid[s][64:96, :].bitcast(F32), 0.0))
                dve.memset(rstd[s][:, :], 0.0).then_inc(stored[s].sem, 16)
            dve.wait_ge(loaded, 16 * LOADS)
            for n, (r, name) in enumerate([(wq_r, "wq"), (wkv_r, "wkv"), (wo_r, "wo"), (wfc_r, "wfc"),
                                           (wproj_r, "wproj"), (wqkvb_r, "wqkvb"), (wout_r, "wout")]):
                dve.wait_ge(prep_hi, n + 1)
                ins = dve.tensor_tensor(r[1][:, :, :].rearrange("p a n -> p (a n)"), raw_at[name],
                                  r[0][:, :, :].rearrange("p a n -> p (a n)").bitcast(F32), ALU.subtract)
            chunks = [(raw_at["gate"][:, 768 * c:768 * c + 768], gate8[:, c, :]) for c in range(2)]
            chunks += [(raw_at["up"][:, 768 * c:768 * c + 768], up8[:, c, :]) for c in range(2)]
            chunks += [(raw_down[c][:, :, :].rearrange("p a n -> p (a n)")[:, 0:768],
                        down8[:, 3 * c:3 * c + 3, :].rearrange("p a n -> p (a n)")) for c in range(2)]
            for raw, q8 in chunks:
                then(dve.tensor_scalar(grid.bitcast(I32), raw.bitcast(I32), 0x7F800000, None, ALU.bitwise_and))
                then(dve.tensor_scalar(grid, grid, 2.0 ** -6, 1.5 * 2.0 ** 20, ALU.max, ALU.mult))
                then(dve.tensor_tensor(raw, raw, grid, ALU.add))
                then(dve.tensor_tensor(q8, raw, grid, ALU.subtract))
                then(dve.tensor_scalar(raw, q8.bitcast(F32), 7.59e35, 0.0, ALU.mult, ALU.mult))
                then(dve.tensor_tensor(q8, q8.bitcast(F32), raw, ALU.add))
            assert done[0] == 42

            dve.wait_ge(const_ready, 2)
            steps = [0]

            with dve.Fori(0, TURNS) as turn:
                def link(ins, alone=False):
                    steps[0] += 1
                    ins.then_inc(vlink.sem, 1)
                    dve.wait_ge(vlink.sem, vlink.at(turn, steps[0]))
                    if alone:
                        dve.sem_inc(passed, 1)

                def flat(ap):
                    return ap.rearrange("p k n -> p (k n)")

                for stage, s in ORDER:
                    if stage.startswith("ln"):
                        n = int(stage[2])
                        if n == 0:
                            dve.wait_ge(x_loaded[s].sem, x_loaded[s].at(turn, 1))
                        elif n == 1:
                            dve.wait_ge(normed[s].sem, normed[s].at(turn, 1))
                        else:
                            dve.wait_ge(summed[s].sem, summed[s].at(turn, n - 1))
                        src, dst = (x_in if n == 0 else cur)[s], (cur if n == 0 else h)[s]
                        for i in range(TT):
                            ins = dve.bn_stats(bnst[s][:, i, :], src[:, i, :])
                        link(ins, alone=True)
                        for i in range(TT):
                            ins = dve.bn_aggr(mv[s][:, i, :], bnst[s][:, i, :])
                        ins.then_inc(stats[s].sem, 1)
                        dve.wait_ge(rstd_ok[s].sem, rstd_ok[s].at(turn, n + 1))
                        if n == 1:
                            dve.wait_ge(stored[s].sem, stored[s].at(turn, 0))
                        for i in range(TT):
                            ins = dve.tensor_scalar(dst[:, i, :], src[:, i, :], mv[s][:, i, 0:1], rstd[s][:, i:i + 1],
                                                    ALU.subtract, ALU.mult)
                        ins.then_inc(normed[s].sem, 1)
                    if stage in ("tr1", "tr2"):
                        n = int(stage[2])
                        g, b = col[f"ln{n}_g"], col[f"ln{n}_b"]
                        dve.wait_ge(*filled(turn, stage, s))
                        bank = bank_of(stage, s)
                        for k in range(KT):
                            ins = dve.tensor_scalar(in_full[s][:, k, :], bank[:, S * k:S * k + S], g[:, k:k + 1],
                                                    b[:, k:k + 1], ALU.mult, ALU.add)
                        ins.then_inc(affine[s].sem, 1)
                        dve.wait_ge(inhi[s].sem, inhi[s].at(turn, n))
                        dve.tensor_tensor(in_lo[s][:, :, :], in_full[s][:, :, :], in_hi[s][:, :, :].bitcast(F32),
                                          ALU.subtract).then_inc(inlo[s].sem, 1)
                    if stage in ("tr3", "tr4", "tr5"):
                        n = int(stage[2])
                        dve.wait_ge(*filled(turn, stage, s))
                        bank = bank_of(stage, s)
                        dve.wait_ge(inhi[s].sem, inhi[s].at(turn, n))
                        dve.tensor_tensor(flat(in_lo[s][:, :, :]), bank[:, :], flat(in_hi[s][:, :, :]).bitcast(F32),
                                          ALU.subtract).then_inc(inlo[s].sem, 1)
                    if stage == "q":
                        dve.wait_ge(qhi[s].sem, qhi[s].at(turn, 1))
                        dve.tensor_tensor(wide[s][:, 1024:1536].bitcast(F32R), wide[s][:, 0:512], wide[s][:, 512:1024],
                                          ALU.subtract).then_inc(qlo[s].sem, 1)
                    if stage == "kv":
                        dve.wait_ge(khi[s].sem, khi[s].at(turn, 1))
                        for c in range(2):
                            ins = dve.tensor_tensor(kst[s][32:64, c, :], wide[s][32:64, 1536:1536 + S],
                                                    wide[s][32:64, 1792:1792 + S], ALU.subtract)
                        ins.then_inc(klo[s].sem, 1)
                    if stage == "vt":
                        dve.wait_ge(*filled(turn, stage, s))
                        bank = bank_of(stage, s)
                        dve.tensor_copy(vaug[s][:, :, 0:HD],
                                        bank[:, 0:64].rearrange("p (i n) -> p i n", i=TT)[:, :, 0:HD])\
                            .then_inc(v_ok[s].sem, 1)
                    if stage == "smax":
                        for i in range(12):
                            dve.wait_ge(*filled(turn, stage, s, i))
                            bank = bank_of(stage, s, i)
                            nh = 4 if i < 4 else 2
                            t, h0 = (0, 4 * i) if i < 4 else (1, 2 * (i - 4))
                            ins = dve.reduce_max(m[s][:, t, h0:h0 + nh], bank[:, :].rearrange("p (h n) -> p h n", h=nh),
                                                 axis=AX_X)
                            ins.then_inc(max_ok[s].sem, 1)
                    if stage == "mt":
                        dve.wait_ge(*filled(turn, stage, s))
                        bank = bank_of(stage, s)
                        dve.wait_ge(mhi[s].sem, mhi[s].at(turn, 1))
                        dve.scalar_tensor_tensor(out=mrow[s][:, 1, :], in0=bank[0:HEADS, 0:S], scalar=-1.0,
                                                 in1=mrow[s][:, 0, :].bitcast(F32), op0=ALU.mult, op1=ALU.subtract)\
                            .then_inc(mlo[s].sem, 1)
                    if stage == "pv":
                        for c in range(2):
                            dve.wait_ge(*filled(turn, stage, s, c))
                            bank = bank_of(stage, s, c)
                            if c:
                                dve.wait_ge(att_lo[s].sem, att_lo[s].at(turn, c))
                            link(dve.reciprocal(attmp[s][:, 0, :], bank[:, :]), alone=True)
                            link(dve.stream_shuffle(attmp[s][:, 1, :], attmp[s][:, 0, :],
                                                    mask=[16 + r % 16 for r in range(32)]))
                            dve.tensor_tensor(attmp[s][:, 0, :], bank[:, :], attmp[s][:, 1, :], ALU.mult)\
                                .then_inc(att_full[s].sem, 1)
                            dve.wait_ge(att_hi[s].sem, att_hi[s].at(turn, c + 1))
                            dve.tensor_tensor(mid_lo[s][:, 512 * c:512 * c + 512], attmp[s][:, 0, :],
                                              mid_hi[s][:, 512 * c:512 * c + 512].bitcast(F32), ALU.subtract)\
                                .then_inc(att_lo[s].sem, 1)
                    if stage in ("wo", "proj", "out"):
                        k, n = {"wo": (1, 1), "proj": (2, 2), "out": (3, 4)}[stage]
                        dve.wait_ge(*filled(turn, stage, s))
                        bank = bank_of(stage, s)
                        dve.wait_ge(base_ok[s].sem, base_ok[s].at(turn, k))
                        dve.tensor_tensor(flat(cur[s][:, :, :]), bank[:, :], flat(base[s][:, :, :]), ALU.add)\
                            .then_inc(summed[s].sem, 1)
                    if stage == "fc":
                        for i in range(4):
                            dve.wait_ge(gelu_hi[s].sem, gelu_hi[s].at(turn, i + 1))
                            dve.tensor_tensor(mid_lo[s][:, 512 * i:512 * i + 512], wide[s][:, 512 * i:512 * i + 512],
                                              mid_hi[s][:, 512 * i:512 * i + 512].bitcast(F32), ALU.subtract)\
                                .then_inc(gelu_lo[s].sem, 1)
                    if stage in ("gu1", "gu2"):
                        f = MT_FF * (stage == "gu2")

                        def lo_half(i):
                            dve.wait_ge(fuse_hi[s].sem, fuse_hi[s].at(turn, f + i + 1))
                            dve.tensor_tensor(mid_lo[s][:, S * i:S * i + S], wide[s][:, S * i:S * i + S],
                                              mid_hi[s][:, S * i:S * i + S].bitcast(F32), ALU.subtract)\
                                .then_inc(fuse_lo[s].sem, 1)

                        for i in range(MT_FF):
                            dve.wait_ge(*filled(turn, stage, s, i))
                            bank = bank_of(stage, s, i)
                            dve.wait_ge(silu[s].sem, silu[s].at(turn, f + i + 1))
                            dve.scalar_tensor_tensor(out=wide[s][:, S * i:S * i + S], in0=bank[:, S:2 * S],
                                                     scalar=col["up_scale"][:, i:i + 1],
                                                     in1=wide[s][:, 2048 + S * i:2048 + S * i + S],
                                                     op0=ALU.mult, op1=ALU.mult).then_inc(fused[s].sem, 1)
                            if i:
                                lo_half(i - 1)
                        lo_half(MT_FF - 1)
                    if stage in ("down1", "down2"):
                        dve.wait_ge(*filled(turn, stage, s))
                        bank = bank_of(stage, s)
                        link(dve.tensor_tensor(base[s][:, :, :], bank[:, :].rearrange("p (i n) -> p i n", i=TT),
                                               row["down_scale"].unsqueeze(1).broadcast_to([P, TT, H]), ALU.mult))
                        dst = cur[s] if stage == "down1" else h[s]
                        ins = dve.tensor_tensor(dst[:, :, :], cur[s][:, :, :], base[s][:, :, :], ALU.add)
                        ins.then_inc((summed if stage == "down1" else out_ok)[s].sem, 1)
                    if stage in ("qb", "kb"):
                        k = int(stage == "kb")
                        dve.wait_ge(qkb_hi[s].sem, qkb_hi[s].at(turn, k + 1))
                        dve.tensor_tensor(mid_lo[s][:, 512 * k:512 * k + 512], wide[s][:, 512 * k:512 * k + 512],
                                          mid_hi[s][:, 512 * k:512 * k + 512].bitcast(F32), ALU.subtract)\
                            .then_inc(qkb_lo[s].sem, 1)
                    if stage == "vb":
                        dve.wait_ge(*filled(turn, stage, s))
                        bank = bank_of(stage, s)
                        dve.tensor_tensor(wide[s][:, 1024:1536].rearrange("p (i n) -> p i n", i=TT),
                                          bank[:, :].rearrange("p (i n) -> p i n", i=TT),
                                          row["bvb"].unsqueeze(1).broadcast_to([P, TT, H]), ALU.add)\
                            .then_inc(vb_full[s].sem, 1)
                        dve.wait_ge(vb_hi[s].sem, vb_hi[s].at(turn, 1))
                        dve.tensor_tensor(mid_lo[s][:, 1024:1536], wide[s][:, 1024:1536],
                                          mid_hi[s][:, 1024:1536].bitcast(F32), ALU.subtract).then_inc(vb_lo[s].sem, 1)
                    if stage == "sb":
                        dve.wait_ge(*filled(turn, stage, s))
                        bank = bank_of(stage, s)
                        link(dve.reduce_max(mb[s][:, :], bank[:, :].rearrange("p (i n) -> p i n", i=TT), axis=AX_X))
                        dve.tensor_scalar(nmb[s][:, :], mb[s][:, :], -(H ** -0.5), None, ALU.mult)\
                            .then_inc(sb_max[s].sem, 1)
                        dve.wait_ge(sb_exp[s].sem, sb_exp[s].at(turn, 1))
                        link(dve.reciprocal(rsumb[s][:, :], sumb[s][:, :]))
                        for i in range(TT):
                            ins = dve.tensor_scalar(wide[s][:, 4608 + S * i:4608 + S * i + S],
                                                    wide[s][:, 4096 + S * i:4096 + S * i + S],
                                                    rsumb[s][:, i:i + 1], None, ALU.mult)
                        ins.then_inc(sb_norm[s].sem, 1)
                    if stage == "pt":
                        dve.wait_ge(*filled(turn, stage, s))
                        bank = bank_of(stage, s)
                        dve.wait_ge(pt_hi[s].sem, pt_hi[s].at(turn, 1))
                        dve.tensor_tensor(mid_lo[s][:, 1536:2048], bank[:, :], mid_hi[s][:, 1536:2048].bitcast(F32),
                                          ALU.subtract).then_inc(pt_lo[s].sem, 1)
                    if stage == "ctx":
                        dve.wait_ge(*filled(turn, stage, s))
                        bank = bank_of(stage, s)
                        dve.wait_ge(ctx_hi[s].sem, ctx_hi[s].at(turn, 1))
                        dve.tensor_tensor(flat(in_lo[s][:, :, :]), bank[:, :], flat(in_hi[s][:, :, :]).bitcast(F32),
                                          ALU.subtract).then_inc(ctx_lo[s].sem, 1)
            assert steps[0] == VLINKS, steps

        @block.tensor
        def _(pe):
            pe.wait_ge(const_ready, 2)
            pe.wait_ge(prep_hi, 7)
            pe.wait_ge(prep, 42)

            def series(out_ap, terms):
                for n, (sta, mov) in enumerate(terms):
                    ins = pe.matmul(out_ap, sta, mov, start=(n == 0), stop=(n == len(terms) - 1))
                return ins

            with pe.Fori(0, TURNS) as turn:
                for stage, s in ORDER:
                    ihi = [in_hi[s][:, k, :] for k in range(KT)]
                    ilo = [in_lo[s][:, k, :] for k in range(KT)]

                    if stage.startswith("tr"):
                        n = int(stage[2])
                        pe.wait_ge(normed[s].sem, normed[s].at(turn, n + 1))
                        pe.wait_ge(*emptied(turn, stage, s))
                        bank, full = bank_of(stage, s), fills_of(stage, s)
                        for k in range(KT):
                            for i in range(TT):
                                ins = pe.transpose(bank[:, S * k + P * i:S * k + P * i + P],
                                                   h[s][:, i, P * k:P * k + P], ident[:, :])
                        ins.then_inc(full, 1)
                    if stage == "q":
                        pe.wait_ge(inhi[s].sem, inhi[s].at(turn, 1))
                        pe.wait_ge(inlo[s].sem, inlo[s].at(turn, 1))
                        pe.wait_ge(*emptied(turn, stage, s))
                        bank, full = bank_of(stage, s), fills_of(stage, s)
                        for t in range(KT):
                            c = slice(P * t, P * t + P)
                            terms = []
                            for k in range(KT):
                                terms += [(wq_r[0][:, k, c], ihi[k]), (wq_r[0][:, k, c], ilo[k]), (wq_r[1][:, k, c], ihi[k])]
                            ins = series(bank[:, S * t:S * t + S], terms)
                        ins.then_inc(full, 1)
                    if stage == "kv":
                        pe.wait_ge(*emptied(turn, stage, s))
                        bank, full = bank_of(stage, s), fills_of(stage, s)
                        terms = []
                        for k in range(KT):
                            terms += [(wkv_r[0][:, k, :], ihi[k]), (wkv_r[0][:, k, :], ilo[k]), (wkv_r[1][:, k, :], ihi[k])]
                        series(bank[0:STACK, 0:S], terms).then_inc(full, 1)
                    if stage == "vt":
                        pe.wait_ge(kvfull[s].sem, kvfull[s].at(turn, 1))
                        pe.sem_inc(passed, 1)
                        pe.wait_ge(*emptied(turn, stage, s))
                        bank, full = bank_of(stage, s), fills_of(stage, s)
                        for i in range(TT):
                            ins = pe.transpose(bank[:, 32 * i:32 * i + 32], wide[s][64:96, 1536 + P * i:1536 + P * i + P],
                                               ident[64:96, 64:96])
                        ins.then_inc(full, 1)
                    if stage == "smax":
                        pe.wait_ge(q_stack[s].sem, q_stack[s].at(turn, 4))
                        pe.wait_ge(khi[s].sem, khi[s].at(turn, 1))
                        pe.wait_ge(klo[s].sem, klo[s].at(turn, 1))
                        for i in range(12):
                            pe.wait_ge(*emptied(turn, stage, s, i))
                            bank, full = bank_of(stage, s, i), fills_of(stage, s, i)
                            nh = 4 if i < 4 else 2
                            t, h0 = (0, 4 * i) if i < 4 else (1, 2 * (i - 4))
                            keys = P * (t + 1)
                            for j in range(nh):
                                pe.matmul(bank[:, keys * j:keys * j + keys], qst[s][0:STACK, h0 + j, P * t:P * t + P],
                                          kst[s][:, 0, 0:keys], start=(j == 0), stop=False)
                            pe.matmul(bank[:, :].rearrange("p (h n) -> p h n", h=nh)[:, :, keys - P:keys], ident_b[:, :],
                                      causal_b[:, :].unsqueeze(1).broadcast_to([P, nh, P]), start=False, stop=True)\
                                .then_inc(full, 1)
                    if stage == "mt":
                        pe.wait_ge(max_ok[s].sem, max_ok[s].at(turn, 12))
                        pe.wait_ge(*emptied(turn, stage, s))
                        bank, full = bank_of(stage, s), fills_of(stage, s)
                        for i in range(TT):
                            ins = pe.transpose(bank[0:HEADS, P * i:P * i + P], m[s][:, i, :], ident[:, :])
                        ins.then_inc(full, 1)
                    if stage == "st":
                        pe.wait_ge(m_rows[s].sem, m_rows[s].at(turn, 1))
                        for i in range(12):
                            pe.wait_ge(*emptied(turn, stage, s, i))
                            bank, full = bank_of(stage, s, i), fills_of(stage, s, i)
                            if i < 8:
                                q_cols, keys = qst[s][0:STACK, 2 * i:2 * i + 2, :], slice(0, P)
                            else:
                                q_cols, keys = qst[s][0:STACK, 4 * (i - 8):4 * (i - 8) + 4, P:2 * P], slice(P, 2 * P)
                            pe.matmul(bank[:, :], kst[s][:, 1, keys], q_cols, start=True, stop=True).then_inc(full, 1)
                    if stage == "pv":
                        pe.wait_ge(v_ok[s].sem, v_ok[s].at(turn, 1))
                        pe.wait_ge(masked[s].sem, masked[s].at(turn, 12))
                        for c in range(2):
                            pe.wait_ge(*emptied(turn, stage, s, c))
                            bank, full = bank_of(stage, s, c), fills_of(stage, s, c)
                            for g in (2 * c, 2 * c + 1):
                                col = S * (g % 2)
                                for j in range(4):
                                    hd = 4 * g + j
                                    pe.matmul(bank[32 * j:32 * j + 32, col:col + S], vaug[s][:, 0, :],
                                              wide[s][:, S * hd:S * hd + S], start=True, stop=False)
                                for j in range(4):
                                    hd = 4 * g + j
                                    ins = pe.matmul(bank[32 * j:32 * j + 32, col + P:col + S], vaug[s][:, 1, :],
                                                    wide[s][:, 4096 + P * hd:4096 + P * hd + P], start=False, stop=True)
                            ins.then_inc(full, 1)
                    if stage == "wo":
                        pe.wait_ge(att_hi[s].sem, att_hi[s].at(turn, 2))
                        pe.wait_ge(att_lo[s].sem, att_lo[s].at(turn, 2))
                        pe.wait_ge(*emptied(turn, stage, s))
                        bank, full = bank_of(stage, s), fills_of(stage, s)
                        for i in range(TT):
                            terms = []
                            for g in range(HGROUPS):
                                a = slice(S * g + P * i, S * g + P * i + P)
                                terms += [(mid_hi[s][:, a], wo_r[0][:, g, :]), (mid_hi[s][:, a], wo_r[1][:, g, :]),
                                          (mid_lo[s][:, a], wo_r[0][:, g, :])]
                            ins = series(bank[:, H * i:H * i + H], terms)
                        ins.then_inc(full, 1)
                    if stage == "fc":
                        pe.wait_ge(inhi[s].sem, inhi[s].at(turn, 2))
                        pe.wait_ge(inlo[s].sem, inlo[s].at(turn, 2))
                        for i in range(4):
                            pe.wait_ge(*emptied(turn, stage, s, i))
                            bank, full = bank_of(stage, s, i), fills_of(stage, s, i)
                            for j in range(2):
                                c = slice(P * (2 * i + j), P * (2 * i + j) + P)
                                terms = []
                                for k in range(KT):
                                    terms += [(wfc_r[0][:, k, c], ihi[k]), (wfc_r[0][:, k, c], ilo[k]),
                                              (wfc_r[1][:, k, c], ihi[k])]
                                ins = series(bank[:, S * j:S * j + S], terms)
                            ins.then_inc(full, 1)
                    if stage == "proj":
                        pe.wait_ge(gelu_hi[s].sem, gelu_hi[s].at(turn, 4))
                        pe.wait_ge(gelu_lo[s].sem, gelu_lo[s].at(turn, 4))
                        pe.wait_ge(*emptied(turn, stage, s))
                        bank, full = bank_of(stage, s), fills_of(stage, s)
                        for i in range(TT):
                            terms = []
                            for k in range(MT_FC):
                                a = slice(S * k + P * i, S * k + P * i + P)
                                terms += [(mid_hi[s][:, a], wproj_r[0][:, k, :]), (mid_hi[s][:, a], wproj_r[1][:, k, :]),
                                          (mid_lo[s][:, a], wproj_r[0][:, k, :])]
                            ins = series(bank[:, H * i:H * i + H], terms)
                        ins.then_inc(full, 1)
                    if stage in ("gu1", "gu2"):
                        n = 3 if stage == "gu1" else 5
                        pe.wait_ge(inhi[s].sem, inhi[s].at(turn, n))
                        pe.wait_ge(inlo[s].sem, inlo[s].at(turn, n))
                        for i in range(MT_FF):
                            pe.wait_ge(*emptied(turn, stage, s, i))
                            bank, full = bank_of(stage, s, i), fills_of(stage, s, i)
                            c = slice(P * i, P * i + P)
                            for j, w in enumerate((gate8, up8)):
                                terms = []
                                for k in range(KT):
                                    terms += [(w[:, k, c], ihi[k]), (w[:, k, c], ilo[k])]
                                ins = series(bank[:, S * j:S * j + S], terms)
                            ins.then_inc(full, 1)
                    if stage in ("down1", "down2"):
                        f = MT_FF * (1 + (stage == "down2"))
                        pe.wait_ge(fuse_hi[s].sem, fuse_hi[s].at(turn, f))
                        pe.wait_ge(fuse_lo[s].sem, fuse_lo[s].at(turn, f))
                        pe.wait_ge(*emptied(turn, stage, s))
                        bank, full = bank_of(stage, s), fills_of(stage, s)
                        for i in range(TT):
                            terms = []
                            for k in range(MT_FF):
                                a = slice(S * k + P * i, S * k + P * i + P)
                                terms += [(mid_hi[s][:, a], down8[:, k, :]), (mid_lo[s][:, a], down8[:, k, :])]
                            ins = series(bank[:, H * i:H * i + H], terms)
                        ins.then_inc(full, 1)
                    if stage in ("qb", "kb"):
                        pe.wait_ge(inhi[s].sem, inhi[s].at(turn, 4))
                        pe.wait_ge(inlo[s].sem, inlo[s].at(turn, 4))
                        pe.wait_ge(*emptied(turn, stage, s))
                        bank, full = bank_of(stage, s), fills_of(stage, s)
                        for j in range(KT):
                            c0 = H * (stage == "kb") + P * j
                            c = slice(c0, c0 + P)
                            terms = []
                            for k in range(KT):
                                terms += [(wqkvb_r[0][:, k, c], ihi[k]), (wqkvb_r[0][:, k, c], ilo[k]),
                                          (wqkvb_r[1][:, k, c], ihi[k])]
                            ins = series(bank[:, S * j:S * j + S], terms)
                        ins.then_inc(full, 1)
                    if stage == "vb":
                        pe.wait_ge(*emptied(turn, stage, s))
                        bank, full = bank_of(stage, s), fills_of(stage, s)
                        c = slice(2 * H, 3 * H)
                        for i in range(TT):
                            a = slice(P * i, P * i + P)
                            terms = []
                            for k in range(KT):
                                terms += [(in_hi[s][:, k, a], wqkvb_r[0][:, k, c]), (in_hi[s][:, k, a], wqkvb_r[1][:, k, c]),
                                          (in_lo[s][:, k, a], wqkvb_r[0][:, k, c])]
                            ins = series(bank[:, H * i:H * i + H], terms)
                        ins.then_inc(full, 1)
                    if stage == "sb":
                        pe.wait_ge(qkb_hi[s].sem, qkb_hi[s].at(turn, 2))
                        pe.wait_ge(qkb_lo[s].sem, qkb_lo[s].at(turn, 2))
                        pe.wait_ge(*emptied(turn, stage, s))
                        bank, full = bank_of(stage, s), fills_of(stage, s)
                        for i in range(TT):
                            terms = []
                            for k in range(KT):
                                a = slice(S * k + P * i, S * k + P * i + P)
                                b = slice(512 + S * k, 512 + S * k + S)
                                terms += [(mid_hi[s][:, a], mid_hi[s][:, b]), (mid_hi[s][:, a], mid_lo[s][:, b]),
                                          (mid_lo[s][:, a], mid_hi[s][:, b])]
                            ins = series(bank[:, S * i:S * i + S], terms)
                        ins.then_inc(full, 1)
                    if stage == "pt":
                        pe.wait_ge(sb_norm[s].sem, sb_norm[s].at(turn, 1))
                        pe.wait_ge(*emptied(turn, stage, s))
                        bank, full = bank_of(stage, s), fills_of(stage, s)
                        for t in range(TT):
                            for i in range(TT):
                                a = 4608 + S * i + P * t
                                ins = pe.transpose(bank[:, S * t + P * i:S * t + P * i + P], wide[s][:, a:a + P], ident[:, :])
                        ins.then_inc(full, 1)
                    if stage == "ctx":
                        for c in (pt_hi, pt_lo, vb_hi, vb_lo):
                            pe.wait_ge(c[s].sem, c[s].at(turn, 1))
                        pe.wait_ge(*emptied(turn, stage, s))
                        bank, full = bank_of(stage, s), fills_of(stage, s)
                        for j in range(KT):
                            terms = []
                            for t in range(TT):
                                v = slice(1024 + H * t + P * j, 1024 + H * t + P * j + P)
                                p_ = slice(1536 + S * t, 1536 + S * t + S)
                                terms += [(mid_hi[s][:, v], mid_hi[s][:, p_]), (mid_hi[s][:, v], mid_lo[s][:, p_]),
                                          (mid_lo[s][:, v], mid_hi[s][:, p_])]
                            ins = series(bank[:, S * j:S * j + S], terms)
                        ins.then_inc(full, 1)
                    if stage == "out":
                        pe.wait_ge(ctx_hi[s].sem, ctx_hi[s].at(turn, 1))
                        pe.wait_ge(ctx_lo[s].sem, ctx_lo[s].at(turn, 1))
                        pe.wait_ge(*emptied(turn, stage, s))
                        bank, full = bank_of(stage, s), fills_of(stage, s)
                        for i in range(TT):
                            a = slice(P * i, P * i + P)
                            terms = []
                            for k in range(KT):
                                terms += [(in_hi[s][:, k, a], wout_r[0][:, k, :]), (in_hi[s][:, k, a], wout_r[1][:, k, :]),
                                          (in_lo[s][:, k, a], wout_r[0][:, k, :])]
                            ins = series(bank[:, H * i:H * i + H], terms)
                        ins.then_inc(full, 1)


def kernel(**inputs):
    import numpy as _np
    import concourse.bacc as _bacc
    from concourse import mybir as _mybir
    from concourse.bass_utils import run_bass_kernel_spmd as _run

    def attn_a(n):
        return _np.asarray(inputs["L0_attn_a_" + n])

    def attn_b(n):
        return _np.asarray(inputs["L0_attn_b_" + n])

    def ffn(n):
        return _np.asarray(inputs["L0_ffn_" + n])

    k_bias, v_bias = attn_a("bkv")[:HD], attn_a("bkv")[HD:]
    parts = {"bq": attn_a("bq"), "bfc": attn_a("bfc"), "bqkb": attn_b("b_qkv")[:2 * H],
             "bkv": _np.concatenate([k_bias] * 4 + [v_bias] * 4),
             "gate_scale": ffn("gate_scale"), "up_scale": ffn("up_scale")}
    parts.update({n: attn_a(n) for n in ("ln1_g", "ln1_b", "ln2_g", "ln2_b")})
    columns = _np.concatenate([parts[n].reshape(k, P).T for n, k in COLUMNS], axis=1)
    rows = _np.stack([attn_a("bo"), attn_a("bproj"), attn_b("b_qkv")[2 * H:], attn_b("b_out"), ffn("down_scale")])
    given = {"x": attn_a("hidden_states"), "columns": columns, "rows": rows}
    given.update({n: attn_a(n) for n in ("wq", "wkv", "wo", "wfc", "wproj")})
    given.update({"w_qkv_t": attn_b("w_qkv").T, "w_out_t": attn_b("w_out").T})
    given.update({n: ffn(n) for n in ("gate_w", "up_w", "down_w")})

    nc = _bacc.Bacc("TRN2", target_bir_lowering=False, num_devices=1)
    arrays, args = {}, []
    for name, v in given.items():
        v = _np.ascontiguousarray(v)
        arrays[f"in_{name}"] = v
        args.append(nc.dram_tensor(f"in_{name}", v.shape, _mybir.dt.from_np(v.dtype), kind="ExternalInput").ap())
    out = nc.dram_tensor("out", (BATCH, S, H), _mybir.dt.float32, kind="ExternalOutput").ap()
    build(nc, *args, out)
    r = _run(nc, [arrays], core_ids=[0])
    return r.results[0]["out"]
```

```python
from contextlib import ExitStack

import concourse.bass as bass
from concourse import mybir

ALU = mybir.AluOpType
ACT = mybir.ActivationFunctionType
AX_X = mybir.AxisListType.X
F32 = mybir.dt.float32
F32R = mybir.dt.float32r
BF16 = mybir.dt.bfloat16
I32 = mybir.dt.int32

P = 128
BATCH, S, H = 8, 256, 256
HEADS, HD = 16, 16
INTER, FF = 1024, 768
KT = H // P
TT = S // P
MT_FC = INTER // P
MT_FF = FF // P
SIDES = 2
TURNS = BATCH // SIDES
EPS = 1e-5
RING = 4
HGROUPS = HEADS // 4
STACK = 96
NEG = -3.0e38

CHAIN_A = ["ln0", "nm0", "ln1", "nm1", "tr1", "q", "kv", "vt", "sm0", "sm1", "sm2", "mt", "st0", "st1", "st2",
           "pv0", "pv1", "ta", "ts", "wo", "ln2", "nm2", "tr2"]
CHAIN_F = ["fc0", "fc1", "fc2", "fc3", "pp0", "pp1", "fl", "pp2", "proj", "ln3", "nm3", "tr3", "gu1.0",
           "gu1.1", "gu1.2", "gu1.3", "gu1.4", "gu1.5", "dp1.0", "gl1", "dp1.1", "down1", "ln4", "nm4", "tr4",
           "qb", "kb", "vb", "sb", "pt", "ctx", "out", "ln5", "nm5", "tr5", "gu2.0", "gu2.1", "gu2.2", "gu2.3",
           "gu2.4", "gu2.5", "dp2.0", "gl2", "dp2.1", "down2"]
MERGE = {
    "pe": "FFFAAFAFFAFAFFAAAFFFFFFFFFAAFFAFFFAFFFFAFFAFFAFFAAAFFAFFFAAFFFAFAFFF",
    "dve": "AFAAFAFFFFFAFFFFAAFFAFFFFFAFFFAAFFAAAFFFFFFFFFAFFAAAFAFFFAAFFAFFFFAF",
    "act": "AFFFFFFAFAAAFAFFAFFFFAAFFFAFFAFFAFFFFFFAFFFAFAFAFAAFFAFAFFFFAFFFFAAF",
    "pool": "FFAFAAAAFAFFFFFAFFFAFFFFAFFFFFFAFFAFFAAAFAAFFFFAFFAAFFFFAAFFFFFFAAFF",
    "sp": "FFAAFFAFAFFFFAAFAFFFFAAFFFAFAFFFFFAFAFAFFFFFFFAAAFFAFFFAFFAFAFAFFAFF",
}

FILLS = {"tr1": 1, "q": 1, "kv": 1, "vt": 1, "sm": 4, "mt": 1, "st": 4, "pv": 1, "ta": 2, "ts": 1, "wo": 1,
         "tr2": 1, "fc": 1, "proj": 1, "tr3": 1, "gu": 1, "down": 1, "tr4": 1, "qb": 1, "kb": 1, "vb": 1,
         "sb": 1, "pt": 1, "ctx": 1, "out": 1, "tr5": 1}


def fills(step):
    return FILLS.get(step, FILLS.get(step[:2], FILLS.get(step[:-1], 0)))


FILL_LIST = [(step, i) for step in CHAIN_A + CHAIN_F for i in range(fills(step))]
FILL_NO = {key: n for n, key in enumerate(FILL_LIST)}
USES = [len(FILL_LIST[b::RING]) for b in range(RING)]

VECTOR_LINKS = {"ln0": 2, "ln1": 2, "ln2": 2, "ln3": 2, "ln4": 2, "ln5": 2, "ta": 2, "down1": 1, "down2": 1,
                "sb": 1}
VECTOR_LINKS.update({f"gu{n}.{i}": 1 for n in (1, 2) for i in range(MT_FF)})
POOL_LINKS = {"tr2": 1}
SCALAR_LINKS = {"q": 1}


def half(number, engine, chains="AF"):
    a, f, plan = iter(CHAIN_A), iter(CHAIN_F), []
    for which in MERGE[engine]:
        step = next(a if which == "A" else f)
        if which in chains:
            side = (number == 2) == (which == "A")
            plan.append((step, int(side), int(number == 1 and which == "F")))
    return plan


def first(engine):
    return half(1, engine, "A") + half(2, engine)


def body(engine):
    return half(1, engine) + half(2, engine)


def last(engine):
    return half(1, engine, "F")


COLUMNS = [("ln1_g", KT), ("ln1_b", KT), ("ln2_g", KT), ("ln2_b", KT), ("bq", KT), ("bkv", 1),
           ("bfc", MT_FC), ("bqkb", 2 * KT), ("gate_scale", MT_FF), ("up_scale", MT_FF)]
ROWS = ["bo", "bproj", "bvb", "bout", "down_scale"]


def build(nc, x, columns, rows, wq, wkv, wo, wfc, wproj, w_qkv_t, w_out_t, gate_w, up_w, down_w, out):
    ctx = ExitStack()
    with ctx:
        def sb(name, shape, dt=F32):
            return ctx.enter_context(nc.sbuf_tensor(name, shape, dt))

        def sem(name):
            return ctx.enter_context(nc.semaphore(name))

        class Count:

            def __init__(self, name, times, each=1):
                self.sem, self.times, self.each = sem(name), times, each

            def at(self, when, k):
                turn, lag = when
                return turn * (self.times * self.each) + (k - lag * self.times) * self.each

        def sides(name, times, each=1):
            return [Count(f"{name}{s}", times, each) for s in range(SIDES)]

        wq_r = [sb(f"wq_{n}", [P, KT, H], F32R) for n in ("hi", "lo")]
        wkv_r = [sb(f"wkv_{n}", [P, KT, STACK], F32R) for n in ("hi", "lo")]
        wo_r = [sb(f"wo_{n}", [P, KT, H], F32R) for n in ("hi", "lo")]
        wfc_r = [sb(f"wfc_{n}", [P, KT, INTER], F32R) for n in ("hi", "lo")]
        wproj_r = [sb(f"wproj_{n}", [P, MT_FC, H], F32R) for n in ("hi", "lo")]
        wqkvb_r = [sb(f"wqkvb_{n}", [P, KT, 3 * H], F32R) for n in ("hi", "lo")]
        wout_r = [sb(f"wout_{n}", [P, KT, H], F32R) for n in ("hi", "lo")]
        gate8 = sb("gate8", [P, KT, FF], F32R)
        up8 = sb("up8", [P, KT, FF], F32R)
        down8 = sb("down8", [P, MT_FF, H], F32R)

        col_table = sb("columns", [P, sum(n for _, n in COLUMNS)])
        row_table = sb("rows", [P, len(ROWS), H])
        col, at = {}, 0
        for name, n in COLUMNS:
            col[name] = col_table[:, at:at + n]
            at += n
        row = {name: row_table[:, r, :] for r, name in enumerate(ROWS)}

        half_gs = sb("half_gs", [P, MT_FF])
        half_gs_us = sb("half_gs_us", [P, MT_FF])

        ident = sb("ident", [P, P])
        ident_b = sb("ident_b", [P, P], BF16)
        causal_b = sb("causal_b", [P, P], BF16)
        neg_half = sb("neg_half", [P, TT])

        def each_side(name, shape, dt=F32):
            return [sb(f"{name}{s}", shape, dt) for s in range(SIDES)]

        x_in = each_side("x_in", [P, TT, H])
        cur = each_side("cur", [P, TT, H])
        h = each_side("h", [P, TT, H])
        base = each_side("base", [P, TT, H])
        in_full = each_side("in_full", [P, KT, S])
        in_hi = each_side("in_hi", [P, KT, S], F32R)
        in_lo = each_side("in_lo", [P, KT, S], F32R)
        wide = each_side("wide", [P, 24 * S])
        mid = each_side("mid", [P, 16 * S], F32R)
        kst = each_side("kst", [STACK, 2, S], F32R)
        vaug = each_side("vaug", [P, TT, 32])
        m = each_side("m", [P, TT, HEADS])
        attmp = each_side("attmp", [P, 2, 2 * S])
        rden = each_side("rden", [P, TT, HEADS])
        bnst = each_side("bnst", [P, TT, 6])
        mv = each_side("mv", [P, TT, 2])
        veps = each_side("veps", [P, TT])
        rstd = each_side("rstd", [P, TT])
        mb = each_side("mb", [P, TT])
        nmb = each_side("nmb", [P, TT])
        sumb = each_side("sumb", [P, TT])
        rsumb = each_side("rsumb", [P, TT])

        qst = [mid[s][:, :].rearrange("p (h s) -> p h s", h=HEADS) for s in range(SIDES)]
        mrow = [in_lo[s][0:HEADS, :, :] for s in range(SIDES)]
        mid_hi = [mid[s][:, 0:8 * S] for s in range(SIDES)]
        mid_lo = [mid[s][:, 8 * S:16 * S] for s in range(SIDES)]
        q_scr = nc.dram_tensor("q_scr", (SIDES, 2, H, S), F32, kind="Internal").ap()

        m_scr = nc.dram_tensor("m_scr", (SIDES, 2, HEADS, S), F32, kind="Internal").ap()

        ps = [[ctx.enter_context(nc.psum_tensor(f"bank{s}{b}", [P, 512], F32)) for b in range(RING)]
              for s in range(SIDES)]

        loaded = {n: sem(f"loaded_{n}") for n in ("columns", "rows", "wq", "wkv", "wo", "wfc", "wproj", "gate",
                                                  "wout", "up", "down", "wqkvb")}
        ready = {n: sem(f"ready_{n}") for n in ("wq", "wkv", "wo", "wfc", "wproj", "gate", "wout", "up", "down",
                                                "wqkvb")}
        x_loaded = sides("x_loaded", 1, 16)
        x_in_free = sides("x_in_free", 1)
        stored = sides("stored", 1, 16)
        const_ready = sem("const_ready")
        const_step = sem("const_step")
        cols_ready = sem("cols_ready")
        prep_hi = sem("prep_hi")
        prep_step = sem("prep_step")
        passed = sem("passed")
        bank_full = [[sem(f"bank_full{s}{b}") for b in range(RING)] for s in range(SIDES)]
        vector_step = sides("vector_step", sum(VECTOR_LINKS.values()))
        pool_step = sides("pool_step", sum(POOL_LINKS.values()))
        scalar_step = sides("scalar_step", sum(SCALAR_LINKS.values()))

        stats = sides("stats", 6)
        rstd_ok = sides("rstd_ok", 6)
        normed = sides("normed", 6)
        affine = sides("affine", 2)
        inhi = sides("inhi", 6)
        inlo = sides("inlo", 6)
        qhi = sides("qhi", 1)
        qlo = sides("qlo", 1)
        q_out = sides("q_out", 2, 16)
        q_stack = sides("q_stack", 4, 16)
        kvfull = sides("kvfull", 1)
        khi = sides("khi", 1)
        klo = sides("klo", 1)
        v_ok = sides("v_ok", 1)
        max_ok = sides("max_ok", 12)
        mhi = sides("mhi", 1)
        mlo = sides("mlo", 1)
        m_out = sides("m_out", 1, 16)
        m_rows = sides("m_rows", 1, 16)
        exped = sides("exped", 12)
        masked = sides("masked", 12)
        att_raw = sides("att_raw", 2)
        att_ok = sides("att_ok", 2)
        base_ok = sides("base_ok", 3)
        summed = sides("summed", 4)
        out_ok = sides("out_ok", 1)
        gelu = sides("gelu", 4)
        gelu_hi = sides("gelu_hi", 4)
        gelu_lo = sides("gelu_lo", 4)
        tanh_ok = sides("tanh_ok", 2 * MT_FF)
        fused = sides("fused", 2 * MT_FF)
        fuse_hi = sides("fuse_hi", 2 * MT_FF)
        fuse_lo = sides("fuse_lo", 2 * MT_FF)
        qkb_full = sides("qkb_full", 2)
        qkb_hi = sides("qkb_hi", 2)
        qkb_lo = sides("qkb_lo", 2)
        vb_full = sides("vb_full", 1)
        vb_hi = sides("vb_hi", 1)
        vb_lo = sides("vb_lo", 1)
        sb_max = sides("sb_max", 1)
        sb_exp = sides("sb_exp", 1)
        sb_norm = sides("sb_norm", 1)
        pt_hi = sides("pt_hi", 1)
        pt_lo = sides("pt_lo", 1)
        ctx_hi = sides("ctx_hi", 1)
        ctx_lo = sides("ctx_lo", 1)

        SPLIT_NO = {"tr1": 1, "ts": 2, "tr2": 3, "tr3": 4, "tr4": 5, "tr5": 6}

        def bank_of(step, s, i=0):
            return ps[s][FILL_NO[(step, i)] % RING]

        def fills_of(step, s, i=0):
            return bank_full[s][FILL_NO[(step, i)] % RING]

        def filled(when, step, s, i=0):
            n = FILL_NO[(step, i)]
            turn, lag = when
            uses = USES[n % RING]
            return bank_full[s][n % RING], turn * uses + (n // RING + 1 - lag * uses)

        def last_read(step, s, i):
            name, part = (step[:2], step[2:]) if step[:2] in ("sm", "st", "fc", "gu", "pv") else (step, "0")
            if name == "gu":
                return fused[s], MT_FF * (part[0] == "2") + int(part[2]) + 1
            return {"tr1": (affine[s], 1), "tr2": (affine[s], 2), "ts": (inlo[s], 2), "tr3": (inlo[s], 4),
                    "tr4": (inlo[s], 5), "tr5": (inlo[s], 6), "q": (qhi[s], 1), "kv": (kvfull[s], 1),
                    "vt": (v_ok[s], 1), "sm": (max_ok[s], 4 * int(part) + i + 1), "mt": (mlo[s], 1),
                    "st": (exped[s], 4 * int(part) + i + 1), "pv": (att_raw[s], int(part) + 1),
                    "ta": (att_ok[s], i + 1), "wo": (summed[s], 1), "proj": (summed[s], 2),
                    "fc": (gelu_hi[s], int(part) + 1), "down1": (summed[s], 3), "qb": (qkb_full[s], 1),
                    "kb": (qkb_full[s], 2), "vb": (vb_full[s], 1), "sb": (sb_exp[s], 1), "pt": (pt_lo[s], 1),
                    "ctx": (ctx_lo[s], 1), "out": (summed[s], 4), "down2": (out_ok[s], 1)}[name]

        def emptied(when, step, s, i=0):
            n = FILL_NO[(step, i)]
            if n >= RING:
                count, k = last_read(FILL_LIST[n - RING][0], s, FILL_LIST[n - RING][1])
                return count.sem, count.at(when, k)
            turn, lag = when
            if isinstance(turn, int) and turn == lag:
                return const_ready, 1
            before = FILL_LIST[n + RING * (USES[n % RING] - 1)]
            count, k = last_read(before[0], s, before[1])
            return count.sem, count.at((turn, lag + 1), k)

        def link_at(links, count, when, step, k):
            before = 0
            for name in CHAIN_A + CHAIN_F:
                if name == step:
                    break
                before += links.get(name, 0)
            assert k <= links[step]
            return count.at(when, before + k)

        def flat(t):
            return t[:, :, :].rearrange("p a n -> p (a n)")

        raw = {"wq": flat(attmp[1])[:, 0:512], "wo": flat(attmp[1])[:, 512:1024],
               "wkv": flat(in_full[1])[:, 0:KT * STACK],
               "wfc": wide[1][:, 0:2048], "wproj": wide[1][:, 2048:4096],
               "gate": wide[1][:, 4096:5632], "wout": wide[1][:, 5632:6144],
               "up": wide[1][:, 0:1536], "down": wide[1][:, 2048:3584], "wqkvb": wide[1][:, 4096:5632]}
        split = {"wq": wq_r, "wkv": wkv_r, "wo": wo_r, "wfc": wfc_r, "wproj": wproj_r, "wout": wout_r,
                 "wqkvb": wqkvb_r}
        rounded = {"gate": gate8, "up": up8, "down": down8}
        grid = flat(base[1])
        PREP_AFTER = {"vt": ["wo", "wfc", "wproj"], "mt": ["gate", "wout"], "st2": ["up"], "ts": ["down"],
                      "tr2": ["wqkvb"]}

        block = ctx.enter_context(nc.Block())

        @block.sync
        def _(sp):
            def load(name, dst, src):
                sp.dma_start(dst, src).then_inc(loaded[name], 16)

            def tiles(ap):
                return ap.rearrange("(k p) n -> p k n", p=P)

            def as3(ap, k):
                return ap.rearrange("p (k n) -> p k n", k=k)

            sp.dma_start(x_in[0][:, :, :], x[0].rearrange("(i p) n -> p i n", p=P)).then_inc(x_loaded[0].sem, 16)
            load("columns", col_table[:, :], columns)
            load("wq", as3(raw["wq"], KT), tiles(wq))
            for r in range(6):
                part = tiles(wkv)[:, :, 0:HD] if r < 4 else tiles(wkv)[:, :, HD:2 * HD]
                load("wkv", as3(raw["wkv"], KT)[:, :, 16 * r:16 * r + 16], part)
            load("wo", as3(raw["wo"], KT), tiles(wo))
            load("rows", row_table[:, :, :], rows.partition_broadcast(P))
            load("wfc", as3(raw["wfc"], KT), tiles(wfc))
            load("wproj", as3(raw["wproj"], MT_FC), tiles(wproj))
            load("gate", as3(raw["gate"], KT), tiles(gate_w))
            load("wout", as3(raw["wout"], KT), tiles(w_out_t))
            sp.dma_start(x_in[1][:, :, :], x[1].rearrange("(i p) n -> p i n", p=P)).then_inc(x_loaded[1].sem, 16)

            def steps(turn, plan):
                for step, s, lag in plan:
                    when = (turn, lag)
                    if step == "kv":
                        sp.wait_ge(qhi[s].sem, qhi[s].at(when, 1))
                        sp.dma_start(tiles(q_scr[s, 0]), as3(wide[s][:, 512:1024], KT)).then_inc(q_out[s].sem, 16)
                        sp.wait_ge(qlo[s].sem, qlo[s].at(when, 1))
                        sp.dma_start(tiles(q_scr[s, 1]), as3(wide[s][:, 1024:1536], KT)).then_inc(q_out[s].sem, 16)
                        sp.wait_ge(q_out[s].sem, q_out[s].at(when, 2))
                        for r in range(4):
                            sp.dma_start(qst[s][16 * r:16 * r + 16, :, :].bitcast(F32),
                                         q_scr[s, r % 2].rearrange("(h d) n -> d h n", d=HD))\
                                .then_inc(q_stack[s].sem, 16)
                        if isinstance(turn, int) and turn == 0 and s == 0:
                            for name, before, k, src in (("up", "wfc", KT, up_w), ("down", "wproj", MT_FF, down_w)):
                                sp.wait_ge(ready[before], 1)
                                load(name, as3(raw[name], k), tiles(src))
                    if step == "mt":
                        sp.wait_ge(mlo[s].sem, mlo[s].at(when, 1))
                        sp.dma_start(m_scr[s].rearrange("c h n -> h c n"), mrow[s].bitcast(F32))\
                            .then_inc(m_out[s].sem, 16)
                        sp.wait_ge(m_out[s].sem, m_out[s].at(when, 1))
                        sp.dma_start(mid[s][64:66, :].bitcast(F32), m_scr[s].rearrange("c h n -> c (h n)"))\
                            .then_inc(m_rows[s].sem, 16)
                        if isinstance(turn, int) and turn == 0 and s == 0:
                            sp.wait_ge(ready["gate"], 1)
                            load("wqkvb", as3(raw["wqkvb"], KT), tiles(w_qkv_t))
                    if step == "down2" and s == 1:
                        sp.wait_ge(out_ok[s].sem, out_ok[s].at(when, 1))
                        sp.dma_start(out_tiles(turn - 1, s), h[s][:, :, :]).then_inc(stored[s].sem, 16)

            def tile_of(ap, turn, s):
                return ap[bass.ds(turn * SIDES + s, 1)].rearrange("a (i p) n -> p (a i) n", p=P)

            def out_tiles(turn, s):
                return tile_of(out, turn, s)

            def store_side_0(turn):
                sp.wait_ge(out_ok[0].sem, out_ok[0].at((turn, 1), 1))
                sp.dma_start(out_tiles(turn - 1, 0), h[0][:, :, :]).then_inc(stored[0].sem, 16)

            steps(0, first("sp"))
            with sp.Fori(1, TURNS) as turn:
                for s in range(SIDES):
                    sp.wait_ge(x_in_free[s].sem, x_in_free[s].at((turn, 1), 1))
                    sp.dma_start(x_in[s][:, :, :], tile_of(x, turn, s)).then_inc(x_loaded[s].sem, 16)
                store_side_0(turn)
                steps(turn, body("sp"))
            store_side_0(TURNS)
            steps(TURNS, last("sp"))
            for s in range(SIDES):
                sp.wait_ge(stored[s].sem, 16 * TURNS)

        @block.gpsimd
        def _(pool):
            pool.memset(neg_half[:, :], -0.5)
            pool.memset(ident[:, :], 0.0)
            pool.memset(ident_b[:, :], 0.0)
            pool.memset(causal_b[:, :], 0.0).then_inc(const_step, 1)
            pool.wait_ge(const_step, 1)
            for t in (ident, ident_b):
                pool.affine_select(out=t[:, :], in_=t[:, :], compare_op=ALU.not_equal, fill=1.0, base=0,
                                   pattern=[[-1, P]], channel_multiplier=1)
            pool.affine_select(out=causal_b[:, :], in_=causal_b[:, :], compare_op=ALU.is_ge, fill=NEG, base=0,
                               pattern=[[-1, P]], channel_multiplier=1).then_inc(const_ready, 1)
            pool.wait_ge(const_ready, 1)
            pool.wait_ge(loaded["rows"], 16)

            def steps(turn, plan):
                for step, s, lag in plan:
                    when = (turn, lag)

                    def add_row(name):
                        return pool.tensor_tensor(base[s][:, :, :], cur[s][:, :, :],
                                                  row[name].unsqueeze(1).broadcast_to([P, TT, H]), ALU.add)

                    if step.startswith("ln"):
                        n = int(step[2])
                        pool.wait_ge(stats[s].sem, stats[s].at(when, n + 1))
                        pool.tensor_tensor(rstd[s][:, :], veps[s][:, :], neg_half[:, :], ALU.pow)\
                            .then_inc(rstd_ok[s].sem, 1)
                    if step == "tr1":
                        pool.wait_ge(normed[s].sem, normed[s].at(when, 1))
                        add_row("bo").then_inc(base_ok[s].sem, 1)
                    if step == "tr2":
                        pool.wait_ge(summed[s].sem, summed[s].at(when, 1))
                        add_row("bproj").then_inc(pool_step[s].sem, 1)
                        pool.wait_ge(pool_step[s].sem, link_at(POOL_LINKS, pool_step[s], when, step, 1))
                        pool.tensor_tensor(base[s][:, :, :], base[s][:, :, :], x_in[s][:, :, :], ALU.add)\
                            .then_inc(base_ok[s].sem, 1)
                        pool.wait_ge(base_ok[s].sem, base_ok[s].at(when, 2))
                        pool.sem_inc(x_in_free[s].sem, 1)
                    if step == "tr4":
                        pool.wait_ge(summed[s].sem, summed[s].at(when, 3))
                        add_row("bout").then_inc(base_ok[s].sem, 1)
                    if step[:2] == "st":
                        for i in range(4 * int(step[2]), 4 * int(step[2]) + 4):
                            pool.wait_ge(exped[s].sem, exped[s].at(when, i + 1))
                            pool.sem_inc(passed, 1)
                            nh = 2 if i < 8 else 4
                            v = wide[s][:, 512 * i:512 * i + 512].rearrange("p (h n) -> p h n", h=nh)[:, :, 0:P]
                            pool.affine_select(out=v, in_=v, compare_op=ALU.is_ge, fill=0.0, base=0,
                                               pattern=[[0, nh], [1, P]], channel_multiplier=-1)\
                                .then_inc(masked[s].sem, 1)
                    if step[:2] in ("gu", "gl"):
                        f = MT_FF * (step[2] == "2")
                        i = MT_FF - 1 if step[:2] == "gl" else int(step[4]) - 1
                        if i >= 0:
                            pool.wait_ge(fuse_hi[s].sem, fuse_hi[s].at(when, f + i + 1))
                            pool.tensor_tensor(mid_lo[s][:, S * i:S * i + S], wide[s][:, S * i:S * i + S],
                                               mid_hi[s][:, S * i:S * i + S].bitcast(F32), ALU.subtract)\
                                .then_inc(fuse_lo[s].sem, 1)

            steps(0, first("pool"))
            with pool.Fori(1, TURNS) as turn:
                steps(turn, body("pool"))
            steps(TURNS, last("pool"))

        @block.scalar
        def _(act):
            def prepare(name):
                if name in split:
                    act.wait_ge(loaded[name], 16 * (6 if name == "wkv" else 1))
                    act.activation(flat(split[name][0]), raw[name], ACT.Copy).then_inc(prep_hi, 1)

            def steps(turn, plan, prep=False):
                for step, s, lag in plan:
                    when = (turn, lag)
                    if step in SPLIT_NO:
                        n = SPLIT_NO[step]
                        if step in ("tr1", "tr2"):
                            act.wait_ge(affine[s].sem, affine[s].at(when, int(step[2])))
                            src = flat(in_full[s])
                        else:
                            act.wait_ge(*filled(when, step, s))
                            src = bank_of(step, s)[:, :]
                        act.activation(flat(in_hi[s]), src, ACT.Copy).then_inc(inhi[s].sem, 1)
                    if step == "q":
                        act.wait_ge(*filled(when, step, s))
                        bank = bank_of(step, s)
                        for k in range(KT):
                            ins = act.activation(wide[s][:, S * k:S * k + S], bank[:, S * k:S * k + S],
                                                 ACT.Identity, bias=col["bq"][:, k:k + 1])
                        ins.then_inc(scalar_step[s].sem, 1)
                        act.wait_ge(scalar_step[s].sem, link_at(SCALAR_LINKS, scalar_step[s], when, step, 1))
                        act.activation(wide[s][:, 512:1024].bitcast(F32R), wide[s][:, 0:512], ACT.Copy)\
                            .then_inc(qhi[s].sem, 1)
                    if step == "kv":
                        act.wait_ge(*filled(when, step, s))
                        act.activation(wide[s][0:STACK, 1536:1536 + S], bank_of(step, s)[0:STACK, 0:S], ACT.Identity,
                                       bias=col["bkv"][0:STACK, :]).then_inc(kvfull[s].sem, 1)
                        act.wait_ge(kvfull[s].sem, kvfull[s].at(when, 1))
                        act.activation(kst[s][0:32, :, :],
                                       wide[s][0:32, 1536:1536 + S].unsqueeze(1).broadcast_to([32, 2, S]), ACT.Copy)
                        act.activation(wide[s][32:64, 1792:1792 + S].bitcast(F32R), wide[s][32:64, 1536:1536 + S],
                                       ACT.Copy).then_inc(khi[s].sem, 1)
                    if step == "mt":
                        act.wait_ge(*filled(when, step, s))
                        act.activation(mrow[s][:, 0, :], bank_of(step, s)[0:HEADS, 0:S], ACT.Copy, scale=-1.0)\
                            .then_inc(mhi[s].sem, 1)
                    if step[:2] == "st":
                        for i in range(4):
                            act.wait_ge(*filled(when, step, s, i))
                            c = 512 * (4 * int(step[2]) + i)
                            act.activation(wide[s][:, c:c + 512], bank_of(step, s, i)[:, :], ACT.Exp,
                                           scale=HD ** -0.5).then_inc(exped[s].sem, 1)
                    if step[:2] == "pv":
                        act.wait_ge(*filled(when, step, s))
                        act.activation(attmp[s][:, int(step[2]), :], bank_of(step, s)[:, :], ACT.Copy)\
                            .then_inc(att_raw[s].sem, 1)
                    if step[:2] == "fc":
                        i = int(step[2])
                        act.wait_ge(*filled(when, step, s))
                        bank = bank_of(step, s)
                        for dst, done in ((wide[s], gelu[s]), (mid_hi[s], gelu_hi[s])):
                            for j in range(2):
                                t = 2 * i + j
                                ins = act.activation(dst[:, S * t:S * t + S], bank[:, S * j:S * j + S],
                                                     ACT.Gelu_apprx_tanh, bias=col["bfc"][:, t:t + 1])
                            ins.then_inc(done.sem, 1)
                    if step[:2] in ("gu", "gl"):
                        f = MT_FF * (step[2] == "2")
                        i = MT_FF if step[:2] == "gl" else int(step[4])
                        if i < MT_FF:
                            act.wait_ge(*filled(when, step, s))
                            act.activation(wide[s][:, 2048 + S * i:2048 + S * i + S], bank_of(step, s)[:, 0:S],
                                           ACT.Tanh, scale=half_gs[:, i:i + 1]).then_inc(tanh_ok[s].sem, 1)
                        if i > 0:
                            act.wait_ge(fused[s].sem, fused[s].at(when, f + i))
                            act.activation(mid_hi[s][:, S * (i - 1):S * i], wide[s][:, S * (i - 1):S * i],
                                           ACT.Copy).then_inc(fuse_hi[s].sem, 1)
                    if step in ("qb", "kb"):
                        k = int(step == "kb")
                        act.wait_ge(*filled(when, step, s))
                        bank = bank_of(step, s)
                        for j in range(KT):
                            c = 512 * k + S * j
                            ins = act.activation(wide[s][:, c:c + S], bank[:, S * j:S * j + S], ACT.Identity,
                                                 bias=col["bqkb"][:, KT * k + j:KT * k + j + 1])
                        ins.then_inc(qkb_full[s].sem, 1)
                        act.wait_ge(qkb_full[s].sem, qkb_full[s].at(when, k + 1))
                        act.activation(mid_hi[s][:, 512 * k:512 * k + 512], wide[s][:, 512 * k:512 * k + 512], ACT.Copy)\
                            .then_inc(qkb_hi[s].sem, 1)
                    if step == "vb":
                        act.wait_ge(vb_full[s].sem, vb_full[s].at(when, 1))
                        act.activation(mid_hi[s][:, 1024:1536], wide[s][:, 1024:1536], ACT.Copy)\
                            .then_inc(vb_hi[s].sem, 1)
                    if step == "sb":
                        act.wait_ge(sb_max[s].sem, sb_max[s].at(when, 1))
                        bank = bank_of(step, s)
                        for i in range(TT):
                            ins = act.activation(wide[s][:, 4096 + S * i:4096 + S * i + S], bank[:, S * i:S * i + S],
                                                 ACT.Exp, bias=nmb[s][:, i:i + 1], scale=H ** -0.5,
                                                 accum_out=sumb[s][:, i:i + 1])
                        ins.then_inc(sb_exp[s].sem, 1)
                    if step == "pt":
                        act.wait_ge(*filled(when, step, s))
                        act.activation(mid_hi[s][:, 1536:2048], bank_of(step, s)[:, :], ACT.Copy)\
                            .then_inc(pt_hi[s].sem, 1)
                    if step == "ctx":
                        act.wait_ge(*filled(when, step, s))
                        act.activation(flat(in_hi[s]), bank_of(step, s)[:, :], ACT.Copy).then_inc(ctx_hi[s].sem, 1)
                    if prep and s == 0:
                        for name in PREP_AFTER.get(step, []):
                            prepare(name)

            prepare("wq")
            prepare("wkv")
            act.wait_ge(cols_ready, 1)
            steps(0, half(1, "act", "A"), prep=True)
            steps(0, half(2, "act"))
            with act.Fori(1, TURNS) as turn:
                steps(turn, body("act"))
            steps(TURNS, last("act"))

        @block.vector
        def _(dve):
            prep_steps = [0]

            def then(ins):
                prep_steps[0] += 1
                ins.then_inc(prep_step, 1)
                dve.wait_ge(prep_step, prep_steps[0])

            def prepare(name):
                if name in split:
                    hi, lo = split[name]
                    dve.wait_ge(prep_hi, HI_NO[name])
                    dve.tensor_tensor(flat(lo), raw[name], flat(hi).bitcast(F32), ALU.subtract)\
                        .then_inc(ready[name], 1)
                    return
                dve.wait_ge(loaded[name], 16)
                for c in range(0, 1536, 512):
                    w, q8 = raw[name][:, c:c + 512], flat(rounded[name])[:, c:c + 512]
                    then(dve.tensor_scalar(grid.bitcast(I32), w.bitcast(I32), 0x7F800000, None, ALU.bitwise_and))
                    then(dve.tensor_scalar(grid, grid, 2.0 ** -6, 1.5 * 2.0 ** 20, ALU.max, ALU.mult))
                    then(dve.tensor_tensor(w, w, grid, ALU.add))
                    then(dve.tensor_tensor(q8, w, grid, ALU.subtract))
                    then(dve.tensor_scalar(w, q8.bitcast(F32), 7.59e35, 0.0, ALU.mult, ALU.mult))
                    then(dve.tensor_tensor(q8, q8.bitcast(F32), w, ALU.add))
                dve.sem_inc(ready[name], 1)

            HI_NO = {n: k + 1 for k, n in enumerate(["wq", "wkv", "wo", "wfc", "wproj", "wout", "wqkvb"])}

            def steps(turn, plan, prep=False):
                for step, s, lag in plan:
                    when = (turn, lag)

                    def link(ins, k=1):
                        ins.then_inc(vector_step[s].sem, 1)
                        dve.wait_ge(vector_step[s].sem, link_at(VECTOR_LINKS, vector_step[s], when, step, k))

                    if step[:2] == "ln":
                        n = int(step[2])
                        count, k = {0: (x_loaded[s], 1), 1: (normed[s], 1)}.get(n, (summed[s], n - 1))
                        dve.wait_ge(count.sem, count.at(when, k))
                        src = (x_in if n == 0 else cur)[s]
                        for i in range(TT):
                            ins = dve.bn_stats(bnst[s][:, i, :], src[:, i, :])
                        link(ins)
                        dve.sem_inc(passed, 1)
                        for i in range(TT):
                            ins = dve.bn_aggr(mv[s][:, i, :], bnst[s][:, i, :])
                        link(ins, 2)
                        dve.tensor_scalar(veps[s][:, :], mv[s][:, :, 1], EPS, None, ALU.add).then_inc(stats[s].sem, 1)
                    if step[:2] == "nm":
                        n = int(step[2])
                        if n == 1 and not (isinstance(turn, int) and turn == lag):
                            dve.wait_ge(stored[s].sem, stored[s].at((turn, lag + 1), 1))
                        dve.wait_ge(rstd_ok[s].sem, rstd_ok[s].at(when, n + 1))
                        src, dst = (x_in if n == 0 else cur)[s], (cur if n == 0 else h)[s]
                        for i in range(TT):
                            ins = dve.tensor_scalar(dst[:, i, :], src[:, i, :], mv[s][:, i, 0:1], rstd[s][:, i:i + 1],
                                                    ALU.subtract, ALU.mult)
                        ins.then_inc(normed[s].sem, 1)
                    if step in ("tr1", "tr2"):
                        g, b = col[f"ln{step[2]}_g"], col[f"ln{step[2]}_b"]
                        dve.wait_ge(*filled(when, step, s))
                        bank = bank_of(step, s)
                        for k in range(KT):
                            ins = dve.tensor_scalar(in_full[s][:, k, :], bank[:, S * k:S * k + S], g[:, k:k + 1],
                                                    b[:, k:k + 1], ALU.mult, ALU.add)
                        ins.then_inc(affine[s].sem, 1)
                        dve.wait_ge(inhi[s].sem, inhi[s].at(when, SPLIT_NO[step]))
                        dve.tensor_tensor(flat(in_lo[s]), flat(in_full[s]), flat(in_hi[s]).bitcast(F32),
                                          ALU.subtract).then_inc(inlo[s].sem, 1)
                    if step in ("ts", "tr3", "tr4", "tr5"):
                        dve.wait_ge(inhi[s].sem, inhi[s].at(when, SPLIT_NO[step]))
                        dve.tensor_tensor(flat(in_lo[s]), bank_of(step, s)[:, :], flat(in_hi[s]).bitcast(F32),
                                          ALU.subtract).then_inc(inlo[s].sem, 1)
                    if step == "q":
                        dve.wait_ge(qhi[s].sem, qhi[s].at(when, 1))
                        dve.tensor_tensor(wide[s][:, 1024:1536].bitcast(F32R), wide[s][:, 0:512], wide[s][:, 512:1024],
                                          ALU.subtract).then_inc(qlo[s].sem, 1)
                    if step == "kv":
                        dve.wait_ge(khi[s].sem, khi[s].at(when, 1))
                        for c in range(2):
                            ins = dve.tensor_tensor(kst[s][32:64, c, :], wide[s][32:64, 1536:1536 + S],
                                                    wide[s][32:64, 1792:1792 + S], ALU.subtract)
                        ins.then_inc(klo[s].sem, 1)
                    if step == "vt":
                        dve.wait_ge(*filled(when, step, s))
                        dve.tensor_copy(vaug[s][:, :, 0:HD],
                                        bank_of(step, s)[:, 0:64].rearrange("p (i n) -> p i n", i=TT)[:, :, 0:HD])\
                            .then_inc(v_ok[s].sem, 1)
                    if step[:2] == "sm":
                        part = int(step[2])
                        for i in range(4):
                            dve.wait_ge(*filled(when, step, s, i))
                            nh = 4 if part == 0 else 2
                            t, h0 = (0, 4 * i) if part == 0 else (1, 8 * (part - 1) + 2 * i)
                            dve.reduce_max(m[s][:, t, h0:h0 + nh],
                                           bank_of(step, s, i)[:, :].rearrange("p (h n) -> p h n", h=nh), axis=AX_X)\
                                .then_inc(max_ok[s].sem, 1)
                    if step == "mt":
                        dve.wait_ge(mhi[s].sem, mhi[s].at(when, 1))
                        dve.scalar_tensor_tensor(out=mrow[s][:, 1, :], in0=bank_of(step, s)[0:HEADS, 0:S], scalar=-1.0,
                                                 in1=mrow[s][:, 0, :].bitcast(F32), op0=ALU.mult, op1=ALU.subtract)\
                            .then_inc(mlo[s].sem, 1)
                    if step == "ta":
                        for i in range(TT):
                            dve.wait_ge(*filled(when, step, s, i))
                            out_sum = bank_of(step, s, i)[:, :].rearrange("p (h c) -> p h c", h=HEADS)
                            link(dve.reciprocal(rden[s][:, i, :], out_sum[:, :, HD]), i + 1)
                            dve.tensor_tensor(h[s][:, i, :].rearrange("p (h d) -> p h d", h=HEADS),
                                              out_sum[:, :, 0:HD],
                                              rden[s][:, i, :].unsqueeze(2).broadcast_to([P, HEADS, HD]), ALU.mult)\
                                .then_inc(att_ok[s].sem, 1)
                    if step in ("wo", "proj"):
                        k = {"wo": 1, "proj": 2}[step]
                        dve.wait_ge(*filled(when, step, s))
                        dve.wait_ge(base_ok[s].sem, base_ok[s].at(when, k))
                        dve.tensor_tensor(flat(cur[s]), bank_of(step, s)[:, :], flat(base[s]), ALU.add)\
                            .then_inc(summed[s].sem, 1)
                    if step == "ctx":
                        dve.wait_ge(sb_exp[s].sem, sb_exp[s].at(when, 1))
                        dve.reciprocal(rsumb[s][:, :], sumb[s][:, :]).then_inc(sb_norm[s].sem, 1)
                    if step == "out":
                        dve.wait_ge(*filled(when, step, s))
                        dve.wait_ge(base_ok[s].sem, base_ok[s].at(when, 3))
                        dve.wait_ge(sb_norm[s].sem, sb_norm[s].at(when, 1))
                        for i in range(TT):
                            ins = dve.scalar_tensor_tensor(out=cur[s][:, i, :], in0=bank_of(step, s)[:, H * i:H * i + H],
                                                           scalar=rsumb[s][:, i:i + 1], in1=base[s][:, i, :],
                                                           op0=ALU.mult, op1=ALU.add)
                        ins.then_inc(summed[s].sem, 1)
                    if step[:2] in ("fc", "fl"):
                        i = 3 if step == "fl" else int(step[2]) - 1
                        if i >= 0:
                            c = slice(512 * i, 512 * i + 512)
                            dve.wait_ge(gelu_hi[s].sem, gelu_hi[s].at(when, i + 1))
                            dve.tensor_tensor(mid_lo[s][:, c], wide[s][:, c], mid_hi[s][:, c].bitcast(F32),
                                              ALU.subtract).then_inc(gelu_lo[s].sem, 1)
                    if step[:2] == "gu":
                        f, i = MT_FF * (step[2] == "2"), int(step[4])
                        dve.wait_ge(tanh_ok[s].sem, tanh_ok[s].at(when, f + i + 1))
                        bank = bank_of(step, s)
                        t = wide[s][:, 2048 + S * i:2048 + S * i + S]
                        link(dve.scalar_tensor_tensor(out=t, in0=t, scalar=1.0, in1=bank[:, 0:S],
                                                      op0=ALU.add, op1=ALU.mult))
                        dve.scalar_tensor_tensor(out=wide[s][:, S * i:S * i + S], in0=bank[:, S:2 * S],
                                                 scalar=half_gs_us[:, i:i + 1], in1=t,
                                                 op0=ALU.mult, op1=ALU.mult).then_inc(fused[s].sem, 1)
                    if step in ("down1", "down2"):
                        dve.wait_ge(*filled(when, step, s))
                        link(dve.tensor_tensor(base[s][:, :, :],
                                               bank_of(step, s)[:, :].rearrange("p (i n) -> p i n", i=TT),
                                               row["down_scale"].unsqueeze(1).broadcast_to([P, TT, H]), ALU.mult))
                        dst, done = (cur[s], summed[s]) if step == "down1" else (h[s], out_ok[s])
                        dve.tensor_tensor(dst[:, :, :], cur[s][:, :, :], base[s][:, :, :], ALU.add)\
                            .then_inc(done.sem, 1)
                    if step in ("qb", "kb"):
                        k = int(step == "kb")
                        c = slice(512 * k, 512 * k + 512)
                        dve.wait_ge(qkb_hi[s].sem, qkb_hi[s].at(when, k + 1))
                        dve.tensor_tensor(mid_lo[s][:, c], wide[s][:, c], mid_hi[s][:, c].bitcast(F32),
                                          ALU.subtract).then_inc(qkb_lo[s].sem, 1)
                    if step == "vb":
                        dve.wait_ge(*filled(when, step, s))
                        dve.tensor_tensor(wide[s][:, 1024:1536].rearrange("p (i n) -> p i n", i=TT),
                                          bank_of(step, s)[:, :].rearrange("p (i n) -> p i n", i=TT),
                                          row["bvb"].unsqueeze(1).broadcast_to([P, TT, H]), ALU.add)\
                            .then_inc(vb_full[s].sem, 1)
                    if step == "sb":
                        dve.wait_ge(*filled(when, step, s))
                        link(dve.reduce_max(mb[s][:, :], bank_of(step, s)[:, :].rearrange("p (i n) -> p i n", i=TT),
                                            axis=AX_X))
                        dve.tensor_scalar(nmb[s][:, :], mb[s][:, :], -(H ** -0.5), None, ALU.mult)\
                            .then_inc(sb_max[s].sem, 1)
                        dve.wait_ge(vb_hi[s].sem, vb_hi[s].at(when, 1))
                        dve.tensor_tensor(mid_lo[s][:, 1024:1536], wide[s][:, 1024:1536],
                                          mid_hi[s][:, 1024:1536].bitcast(F32), ALU.subtract).then_inc(vb_lo[s].sem, 1)
                    if step == "pt":
                        dve.wait_ge(pt_hi[s].sem, pt_hi[s].at(when, 1))
                        dve.tensor_tensor(mid_lo[s][:, 1536:2048], bank_of(step, s)[:, :],
                                          mid_hi[s][:, 1536:2048].bitcast(F32), ALU.subtract).then_inc(pt_lo[s].sem, 1)
                    if step == "ctx":
                        dve.wait_ge(ctx_hi[s].sem, ctx_hi[s].at(when, 1))
                        dve.tensor_tensor(flat(in_lo[s]), bank_of(step, s)[:, :], flat(in_hi[s]).bitcast(F32),
                                          ALU.subtract).then_inc(ctx_lo[s].sem, 1)
                    if prep and s == 0:
                        for name in PREP_AFTER.get(step, []):
                            prepare(name)

            for s in range(SIDES):
                dve.memset(vaug[s][:, :, :], 1.0)
                then(dve.memset(kst[s][64:96, :, :].bitcast(F32), 0.0))
                then(dve.memset(kst[s][64:66, 1, :].bitcast(F32), 1.0))
                then(dve.memset(mid[s][64:96, :].bitcast(F32), 0.0))
            dve.wait_ge(loaded["columns"], 16)
            then(dve.tensor_scalar(half_gs[:, :], col["gate_scale"], 0.5, None, ALU.mult))
            dve.tensor_tensor(half_gs_us[:, :], half_gs[:, :], col["up_scale"], ALU.mult).then_inc(cols_ready, 1)
            prepare("wq")
            prepare("wkv")
            steps(0, half(1, "dve", "A"), prep=True)
            steps(0, half(2, "dve"))
            with dve.Fori(1, TURNS) as turn:
                steps(turn, body("dve"))
            steps(TURNS, last("dve"))

        @block.tensor
        def _(pe):
            def series(out_ap, terms, first=True, last=True):
                for n, (sta, mov) in enumerate(terms):
                    ins = pe.matmul(out_ap, sta, mov, start=(first and n == 0),
                                    stop=(last and n == len(terms) - 1))
                return ins

            def three(sta, mov):
                return [(sta[0], mov[0]), (sta[0], mov[1]), (sta[1], mov[0])]

            NEEDS = {"q": ["wq"], "kv": ["wkv"], "wo": ["wo"], "fc0": ["wfc"], "pp0": ["wproj"],
                     "gu1.0": ["gate", "up"], "dp1.0": ["down"], "qb": ["wqkvb"], "out": ["wout"]}

            def steps(turn, plan):
                for step, s, lag in plan:
                    when = (turn, lag)
                    if isinstance(turn, int) and turn == 0 and s == 0:
                        for name in NEEDS.get(step, []):
                            pe.wait_ge(ready[name], 1)

                    def x_in_tiles(k, cols=slice(0, S)):
                        return in_hi[s][:, k, cols], in_lo[s][:, k, cols]

                    def from_features(w, c, step_bank, col0):
                        terms = []
                        for k in range(KT):
                            terms += three((w[0][:, k, c], w[1][:, k, c]), x_in_tiles(k))
                        return series(step_bank[0:c.stop - c.start, col0:col0 + S], terms)

                    if step in SPLIT_NO:
                        if step == "ts":
                            pe.wait_ge(att_ok[s].sem, att_ok[s].at(when, 2))
                        else:
                            pe.wait_ge(normed[s].sem, normed[s].at(when, int(step[2]) + 1))
                        pe.wait_ge(*emptied(when, step, s))
                        for k in range(KT):
                            for i in range(TT):
                                ins = pe.transpose(bank_of(step, s)[:, S * k + P * i:S * k + P * i + P],
                                                   h[s][:, i, P * k:P * k + P], ident[:, :])
                        ins.then_inc(fills_of(step, s), 1)
                    if step == "q":
                        pe.wait_ge(inlo[s].sem, inlo[s].at(when, 1))
                        pe.wait_ge(*emptied(when, step, s))
                        for t in range(KT):
                            ins = from_features(wq_r, slice(P * t, P * t + P), bank_of(step, s), S * t)
                        ins.then_inc(fills_of(step, s), 1)
                    if step == "kv":
                        pe.wait_ge(*emptied(when, step, s))
                        from_features(wkv_r, slice(0, STACK), bank_of(step, s), 0).then_inc(fills_of(step, s), 1)
                    if step == "vt":
                        pe.wait_ge(*emptied(when, step, s))
                        pe.wait_ge(kvfull[s].sem, kvfull[s].at(when, 1))
                        pe.sem_inc(passed, 1)
                        for i in range(TT):
                            ins = pe.transpose(bank_of(step, s)[:, 32 * i:32 * i + 32],
                                               wide[s][64:96, 1536 + P * i:1536 + P * i + P], ident[64:96, 64:96])
                        ins.then_inc(fills_of(step, s), 1)
                    if step[:2] == "sm":
                        part = int(step[2])
                        if part == 0:
                            pe.wait_ge(q_stack[s].sem, q_stack[s].at(when, 4))
                            pe.wait_ge(khi[s].sem, khi[s].at(when, 1))
                            pe.wait_ge(klo[s].sem, klo[s].at(when, 1))
                        for i in range(4):
                            pe.wait_ge(*emptied(when, step, s, i))
                            bank = bank_of(step, s, i)
                            nh = 4 if part == 0 else 2
                            t, h0 = (0, 4 * i) if part == 0 else (1, 8 * (part - 1) + 2 * i)
                            keys = P * (t + 1)
                            for j in range(nh):
                                pe.matmul(bank[:, keys * j:keys * j + keys], qst[s][0:STACK, h0 + j, P * t:P * t + P],
                                          kst[s][:, 0, 0:keys], start=(j == 0), stop=False)
                            pe.matmul(bank[:, :].rearrange("p (h n) -> p h n", h=nh)[:, :, keys - P:keys], ident_b[:, :],
                                      causal_b[:, :].unsqueeze(1).broadcast_to([P, nh, P]), start=False, stop=True)\
                                .then_inc(fills_of(step, s, i), 1)
                    if step == "mt":
                        pe.wait_ge(max_ok[s].sem, max_ok[s].at(when, 12))
                        pe.wait_ge(*emptied(when, step, s))
                        for i in range(TT):
                            ins = pe.transpose(bank_of(step, s)[0:HEADS, P * i:P * i + P], m[s][:, i, :], ident[:, :])
                        ins.then_inc(fills_of(step, s), 1)
                    if step[:2] == "st":
                        if step == "st0":
                            pe.wait_ge(m_rows[s].sem, m_rows[s].at(when, 1))
                        for i in range(4):
                            pe.wait_ge(*emptied(when, step, s, i))
                            g = 4 * int(step[2]) + i
                            if g < 8:
                                q_cols, keys = qst[s][0:STACK, 2 * g:2 * g + 2, :], slice(0, P)
                            else:
                                q_cols, keys = qst[s][0:STACK, 4 * (g - 8):4 * (g - 8) + 4, P:2 * P], slice(P, 2 * P)
                            pe.matmul(bank_of(step, s, i)[:, :], kst[s][:, 1, keys], q_cols, start=True, stop=True)\
                                .then_inc(fills_of(step, s, i), 1)
                    if step[:2] == "pv":
                        c = int(step[2])
                        if c == 0:
                            pe.wait_ge(v_ok[s].sem, v_ok[s].at(when, 1))
                        pe.wait_ge(masked[s].sem, masked[s].at(when, 10 + 2 * c))
                        pe.wait_ge(*emptied(when, step, s))
                        bank = bank_of(step, s)
                        for g in (2 * c, 2 * c + 1):
                            at = S * (g % 2)
                            for j in range(4):
                                n = S * (4 * g + j)
                                pe.matmul(bank[32 * j:32 * j + 32, at:at + S], vaug[s][:, 0, :], wide[s][:, n:n + S],
                                          start=True, stop=False)
                            for j in range(4):
                                n = 4096 + P * (4 * g + j)
                                ins = pe.matmul(bank[32 * j:32 * j + 32, at + P:at + S], vaug[s][:, 1, :],
                                                wide[s][:, n:n + P], start=False, stop=True)
                        ins.then_inc(fills_of(step, s), 1)
                    if step == "ta":
                        pe.wait_ge(att_raw[s].sem, att_raw[s].at(when, 2))
                        for i in range(TT):
                            pe.wait_ge(*emptied(when, step, s, i))
                            for g in range(HGROUPS):
                                at = S * (g % 2) + P * i
                                ins = pe.transpose(bank_of(step, s, i)[:, P * g:P * g + P],
                                                   attmp[s][:, g // 2, at:at + P], ident[:, :])
                            ins.then_inc(fills_of(step, s, i), 1)
                    if step[:2] == "fc":
                        if step == "fc0":
                            pe.wait_ge(inlo[s].sem, inlo[s].at(when, SPLIT_NO["tr2"]))
                        pe.wait_ge(*emptied(when, step, s))
                        for j in range(2):
                            t = 2 * int(step[2]) + j
                            ins = from_features(wfc_r, slice(P * t, P * t + P), bank_of(step, s), S * j)
                        ins.then_inc(fills_of(step, s), 1)
                    if step[:2] == "pp" or step == "proj":
                        part = 3 if step == "proj" else int(step[2])
                        if part == 0:
                            pe.wait_ge(*emptied(when, "proj", s))
                        pe.wait_ge(gelu_lo[s].sem, gelu_lo[s].at(when, part + 1))
                        for k in (2 * part, 2 * part + 1):
                            for i in range(TT):
                                a = slice(S * k + P * i, S * k + P * i + P)
                                terms = three((mid_hi[s][:, a], mid_lo[s][:, a]), (wproj_r[0][:, k, :], wproj_r[1][:, k, :]))
                                ins = series(bank_of("proj", s)[:, H * i:H * i + H], terms,
                                             first=(k == 0 and i == 0), last=(k == MT_FC - 1 and i == TT - 1))
                        if step == "proj":
                            ins.then_inc(fills_of(step, s), 1)
                    if step[:2] == "gu":
                        i = int(step[4])
                        if i == 0:
                            n = SPLIT_NO["tr3" if step[2] == "1" else "tr5"]
                            pe.wait_ge(inlo[s].sem, inlo[s].at(when, n))
                        pe.wait_ge(*emptied(when, step, s))
                        for j, w in enumerate((gate8, up8)):
                            terms = [(w[:, k, P * i:P * i + P], x_) for k in range(KT) for x_ in x_in_tiles(k)]
                            ins = series(bank_of(step, s)[:, S * j:S * j + S], terms)
                        ins.then_inc(fills_of(step, s), 1)
                    if step[:2] == "dp" or step in ("down1", "down2"):
                        n, part = (int(step[4]), 2) if step[:4] == "down" else (int(step[2]), int(step[4]))
                        if part == 0:
                            pe.wait_ge(*emptied(when, f"down{n}", s))
                        pe.wait_ge(fuse_lo[s].sem, fuse_lo[s].at(when, MT_FF * (n - 1) + 2 * part + 2))
                        for k in (2 * part, 2 * part + 1):
                            for i in range(TT):
                                a = slice(S * k + P * i, S * k + P * i + P)
                                terms = [(mid_hi[s][:, a], down8[:, k, :]), (mid_lo[s][:, a], down8[:, k, :])]
                                ins = series(bank_of(f"down{n}", s)[:, H * i:H * i + H], terms,
                                             first=(k == 0 and i == 0), last=(k == MT_FF - 1 and i == TT - 1))
                        if part == 2:
                            ins.then_inc(fills_of(step, s), 1)
                    if step in ("qb", "kb"):
                        pe.wait_ge(inlo[s].sem, inlo[s].at(when, SPLIT_NO["tr4"]))
                        pe.wait_ge(*emptied(when, step, s))
                        for j in range(KT):
                            c0 = H * (step == "kb") + P * j
                            ins = from_features(wqkvb_r, slice(c0, c0 + P), bank_of(step, s), S * j)
                        ins.then_inc(fills_of(step, s), 1)
                    if step in ("vb", "wo", "out"):
                        w, cols = {"vb": (wqkvb_r, slice(2 * H, 3 * H)), "wo": (wo_r, slice(0, H)),
                                   "out": (wout_r, slice(0, H))}[step]
                        if step == "wo":
                            pe.wait_ge(inlo[s].sem, inlo[s].at(when, SPLIT_NO["ts"]))
                        if step == "out":
                            pe.wait_ge(ctx_lo[s].sem, ctx_lo[s].at(when, 1))
                        pe.wait_ge(*emptied(when, step, s))
                        for i in range(TT):
                            terms = []
                            for k in range(KT):
                                terms += three(x_in_tiles(k, slice(P * i, P * i + P)), (w[0][:, k, cols], w[1][:, k, cols]))
                            ins = series(bank_of(step, s)[:, H * i:H * i + H], terms)
                        ins.then_inc(fills_of(step, s), 1)
                    if step == "sb":
                        pe.wait_ge(qkb_lo[s].sem, qkb_lo[s].at(when, 2))
                        pe.wait_ge(*emptied(when, step, s))
                        for i in range(TT):
                            terms = []
                            for k in range(KT):
                                a = slice(S * k + P * i, S * k + P * i + P)
                                b = slice(512 + S * k, 512 + S * k + S)
                                terms += three((mid_hi[s][:, a], mid_lo[s][:, a]), (mid_hi[s][:, b], mid_lo[s][:, b]))
                            ins = series(bank_of(step, s)[:, S * i:S * i + S], terms)
                        ins.then_inc(fills_of(step, s), 1)
                    if step == "pt":
                        pe.wait_ge(sb_exp[s].sem, sb_exp[s].at(when, 1))
                        pe.wait_ge(*emptied(when, step, s))
                        for t in range(TT):
                            for i in range(TT):
                                a = 4096 + S * i + P * t
                                ins = pe.transpose(bank_of(step, s)[:, S * t + P * i:S * t + P * i + P],
                                                   wide[s][:, a:a + P], ident[:, :])
                        ins.then_inc(fills_of(step, s), 1)
                    if step == "ctx":
                        pe.wait_ge(pt_lo[s].sem, pt_lo[s].at(when, 1))
                        pe.wait_ge(vb_lo[s].sem, vb_lo[s].at(when, 1))
                        pe.wait_ge(*emptied(when, step, s))
                        for j in range(KT):
                            terms = []
                            for t in range(TT):
                                v = slice(1024 + H * t + P * j, 1024 + H * t + P * j + P)
                                q = slice(1536 + S * t, 1536 + S * t + S)
                                terms += three((mid_hi[s][:, v], mid_lo[s][:, v]), (mid_hi[s][:, q], mid_lo[s][:, q]))
                            ins = series(bank_of(step, s)[:, S * j:S * j + S], terms)
                        ins.then_inc(fills_of(step, s), 1)

            pe.wait_ge(const_ready, 1)
            steps(0, first("pe"))
            with pe.Fori(1, TURNS) as turn:
                steps(turn, body("pe"))
            steps(TURNS, last("pe"))


def kernel(**inputs):
    import numpy as _np
    import concourse.bacc as _bacc
    from concourse import mybir as _mybir
    from concourse.bass_utils import run_bass_kernel_spmd as _run

    def attn_a(n):
        return _np.asarray(inputs["L0_attn_a_" + n])

    def attn_b(n):
        return _np.asarray(inputs["L0_attn_b_" + n])

    def ffn(n):
        return _np.asarray(inputs["L0_ffn_" + n])

    k_bias, v_bias = attn_a("bkv")[:HD], attn_a("bkv")[HD:]
    parts = {"bq": attn_a("bq"), "bfc": attn_a("bfc"), "bqkb": attn_b("b_qkv")[:2 * H],
             "bkv": _np.concatenate([k_bias] * 4 + [v_bias] * 4),
             "gate_scale": ffn("gate_scale"), "up_scale": ffn("up_scale")}
    parts.update({n: attn_a(n) for n in ("ln1_g", "ln1_b", "ln2_g", "ln2_b")})
    columns = _np.concatenate([parts[n].reshape(k, P).T for n, k in COLUMNS], axis=1)
    rows = _np.stack([attn_a("bo"), attn_a("bproj"), attn_b("b_qkv")[2 * H:], attn_b("b_out"), ffn("down_scale")])
    given = {"x": attn_a("hidden_states"), "columns": columns, "rows": rows}
    given.update({n: attn_a(n) for n in ("wq", "wkv", "wo", "wfc", "wproj")})
    given.update({"w_qkv_t": attn_b("w_qkv").T, "w_out_t": attn_b("w_out").T})
    given.update({n: ffn(n) for n in ("gate_w", "up_w", "down_w")})

    nc = _bacc.Bacc("TRN2", target_bir_lowering=False, num_devices=1)
    arrays, args = {}, []
    for name, v in given.items():
        v = _np.ascontiguousarray(v)
        arrays[f"in_{name}"] = v
        args.append(nc.dram_tensor(f"in_{name}", v.shape, _mybir.dt.from_np(v.dtype), kind="ExternalInput").ap())
    out = nc.dram_tensor("out", (BATCH, S, H), _mybir.dt.float32, kind="ExternalOutput").ap()
    build(nc, *args, out)
    r = _run(nc, [arrays], core_ids=[0])
    return r.results[0]["out"]
```
